# Optimizing a Trainium2 kernel written in Bass

```python
import numpy as np
import jax
import jax.numpy as jnp

def _softmax(x, axis=-1):
    return jax.nn.softmax(x, axis=axis)

def _gelu(x):
    return jax.nn.gelu(x, approximate=True)

def _silu(x):
    return jax.nn.silu(x)

def _sigmoid(x):
    return jax.nn.sigmoid(x)

def _layernorm(x, axis=-1, eps=1e-05):
    m = jnp.mean(x, axis=axis, keepdims=True)
    v = jnp.var(x, axis=axis, keepdims=True)
    return (x - m) / jnp.sqrt(v + eps)

def _scatter_add(tgt, idx, src, axis=0):
    return tgt.at[idx].add(src)

def _segment_sum(src, seg, n):
    return jax.ops.segment_sum(src, seg, n)
kernel_name = 'mk_gnn_resnorm_d4_gnn_r64_31ce7d'

def setup_inputs(seed: int=0):
    np.random.seed(seed)
    _w = jnp.asarray

    def _rec_inputs():
        import jax
        import jax.numpy as jnp
        _gk = jax.random.key(seed)
        x = -0.000202 + 1 * jax.random.normal(jax.random.fold_in(_gk, 1), (50000, 128), jnp.float32)
        src = jax.random.randint(jax.random.fold_in(_gk, 2), (12500,), 0, 50000, jnp.int32)
        dst = jnp.minimum((50000 * jax.random.uniform(jax.random.fold_in(_gk, 3), (12500,)) ** 2.0).astype(jnp.int32), 49999)
        _o = jnp.argsort(dst, stable=True)
        src = src[_o]
        dst = dst[_o]
        edge_attr_128 = 4.59472e-05 + 1.00006 * jax.random.normal(jax.random.fold_in(_gk, 11), (12500, 128), jnp.float32)
        edge_type_8 = jax.random.randint(jax.random.fold_in(_gk, 13), (12500,), 0, 8, jnp.int32)
        edge_weight = jax.random.uniform(jax.random.fold_in(_gk, 14), (12500,), jnp.float32, 0.0, 0.999998)
        return (x, src, dst, edge_attr_128, edge_type_8, edge_weight)
    x, src, dst, edge_attr_128, edge_type_8, edge_weight = _rec_inputs()

    def _L0_gnn_setup():
        import jax, jax.numpy as jnp
        import numpy as np
        N = 50000
        E = 625000
        D = 128
        DF = 4 * D

        def layernorm(x, gamma, beta, eps=1e-05):
            mu = jnp.mean(x, axis=-1, keepdims=True)
            var = jnp.var(x, axis=-1, keepdims=True)
            return (x - mu) * jax.lax.rsqrt(var + eps) * gamma + beta
        key = jax.random.key(seed)
        ks = jax.random.split(key, 12)
        s = 1.0 / np.sqrt(D)
        sf = 1.0 / np.sqrt(DF)
        return {'x': jax.random.normal(ks[0], (N, D), jnp.float32), 'edge_index': jax.random.randint(ks[1], (2, E), 0, N, jnp.int32), 'edge_attr': jax.random.normal(ks[2], (E, D), jnp.float32), 'g1': jnp.ones((D,), jnp.float32), 'b1': jnp.zeros((D,), jnp.float32), 'g2': jnp.ones((D,), jnp.float32), 'b2': jnp.zeros((D,), jnp.float32), 'eps_gin': jnp.zeros((), jnp.float32), 'Wg1': jax.random.uniform(ks[3], (D, D), jnp.float32, -s, s), 'bg1': jnp.zeros((D,), jnp.float32), 'Wg2': jax.random.uniform(ks[4], (D, D), jnp.float32, -s, s), 'bg2': jnp.zeros((D,), jnp.float32), 'Wf1': jax.random.uniform(ks[5], (D, DF), jnp.float32, -s, s), 'bf1': jnp.zeros((DF,), jnp.float32), 'Wf2': jax.random.uniform(ks[6], (DF, D), jnp.float32, -sf, sf), 'bf2': jnp.zeros((D,), jnp.float32)}
    _L0_gnn_all = _L0_gnn_setup()
    _L0_gnn_in = {k: v for k, v in _L0_gnn_all.items() if k in ('g1', 'b1', 'g2', 'b2', 'eps_gin', 'Wg1', 'bg1', 'Wg2', 'bg2', 'Wf1', 'bf1', 'Wf2', 'bf2')}
    del _L0_gnn_all

    def _L1_gnn_setup():
        import jax, jax.numpy as jnp
        import numpy as np
        N_NODES = 20000
        N_EDGES = 10000
        D_FEAT = 128
        key = jax.random.key(seed)
        k1, k2 = jax.random.split(key)
        edge_index = jax.random.randint(k1, (2, N_EDGES), 0, N_NODES, dtype=jnp.int64 if jax.config.jax_enable_x64 else jnp.int32)
        X = jax.random.normal(k2, (N_NODES, D_FEAT), dtype=jnp.float32)
        eps = jnp.zeros((1,), dtype=jnp.float32)
        return {'edge_index': edge_index, 'X': X, 'num_nodes': N_NODES, 'eps': eps}
    _L1_gnn_all = _L1_gnn_setup()
    _L1_gnn_in = {k: v for k, v in _L1_gnn_all.items() if k in ('eps',)}
    del _L1_gnn_all

    def _L2_gnn_setup():
        import jax, jax.numpy as jnp
        import numpy as np
        N, E, D = (100000, 9375, 128)
        BN_EPS = 1e-05
        key = jax.random.key(seed)
        ks = jax.random.split(key, 8)
        x = jax.random.normal(ks[0], (N, D), dtype=jnp.float32)
        edge_index = jax.random.randint(ks[1], (2, E), 0, N, dtype=jnp.int64)
        eps = jnp.zeros((), dtype=jnp.float32)
        s = 1.0 / np.sqrt(D)
        W1 = jax.random.uniform(ks[2], (D, D), jnp.float32, -s, s)
        b1 = jax.random.uniform(ks[3], (D,), jnp.float32, -s, s)
        gamma = jnp.ones((D,), jnp.float32)
        beta = jnp.zeros((D,), jnp.float32)
        W2 = jax.random.uniform(ks[4], (D, D), jnp.float32, -s, s)
        b2 = jax.random.uniform(ks[5], (D,), jnp.float32, -s, s)
        return {'x': x, 'edge_index': edge_index, 'eps': eps, 'W1': W1, 'b1': b1, 'gamma': gamma, 'beta': beta, 'W2': W2, 'b2': b2}
    _L2_gnn_all = _L2_gnn_setup()
    _L2_gnn_in = {k: v for k, v in _L2_gnn_all.items() if k in ('eps', 'W1', 'b1', 'gamma', 'beta', 'W2', 'b2')}
    del _L2_gnn_all

    def _L3_gnn_setup():
        import jax, jax.numpy as jnp
        import numpy as np
        N = 50000
        E = 12500
        G = 128
        H = 128
        key = jax.random.key(seed)
        ks = jax.random.split(key, 12)
        x = jax.random.normal(ks[0], (N, G), jnp.float32)
        edge_index = jax.random.randint(ks[1], (2, E), 0, N)
        edge_norm = jax.random.uniform(ks[2], (E,), jnp.float32)
        edge_type = jax.random.randint(ks[3], (E,), 0, 8)
        s = 1.0 / np.sqrt(G).astype(np.float32)
        Wq = jax.random.normal(ks[4], (G, H), jnp.float32) * s
        Wk = jax.random.normal(ks[5], (G, H), jnp.float32) * s
        Wv = jax.random.normal(ks[6], (G, H), jnp.float32) * s
        Wskip = jax.random.normal(ks[7], (G, H), jnp.float32) * s
        bq = jax.random.normal(ks[8], (H,), jnp.float32) * 0.01
        bk = jax.random.normal(ks[9], (H,), jnp.float32) * 0.01
        bv = jax.random.normal(ks[10], (H,), jnp.float32) * 0.01
        bskip = jax.random.normal(ks[11], (H,), jnp.float32) * 0.01
        return {'node_features': x, 'edge_index': edge_index, 'edge_norm': edge_norm, 'edge_type': edge_type, 'Wq': Wq, 'bq': bq, 'Wk': Wk, 'bk': bk, 'Wv': Wv, 'bv': bv, 'Wskip': Wskip, 'bskip': bskip}
    _L3_gnn_all = _L3_gnn_setup()
    _L3_gnn_in = {k: v for k, v in _L3_gnn_all.items() if k in ('Wq', 'bq', 'Wk', 'bk', 'Wv', 'bv', 'Wskip', 'bskip')}
    del _L3_gnn_all
    return {'x': x, 'src': src, 'dst': dst, 'edge_attr_128': edge_attr_128, 'edge_type_8': edge_type_8, 'edge_weight': edge_weight, 'L0_gnn_g1': _L0_gnn_in['g1'], 'L0_gnn_b1': _L0_gnn_in['b1'], 'L0_gnn_g2': _L0_gnn_in['g2'], 'L0_gnn_b2': _L0_gnn_in['b2'], 'L0_gnn_eps_gin': _L0_gnn_in['eps_gin'], 'L0_gnn_Wg1': _L0_gnn_in['Wg1'], 'L0_gnn_bg1': _L0_gnn_in['bg1'], 'L0_gnn_Wg2': _L0_gnn_in['Wg2'], 'L0_gnn_bg2': _L0_gnn_in['bg2'], 'L0_gnn_Wf1': _L0_gnn_in['Wf1'], 'L0_gnn_bf1': _L0_gnn_in['bf1'], 'L0_gnn_Wf2': _L0_gnn_in['Wf2'], 'L0_gnn_bf2': _L0_gnn_in['bf2'], 'L1_gnn_eps': _L1_gnn_in['eps'], 'L2_gnn_eps': _L2_gnn_in['eps'], 'L2_gnn_W1': _L2_gnn_in['W1'], 'L2_gnn_b1': _L2_gnn_in['b1'], 'L2_gnn_gamma': _L2_gnn_in['gamma'], 'L2_gnn_beta': _L2_gnn_in['beta'], 'L2_gnn_W2': _L2_gnn_in['W2'], 'L2_gnn_b2': _L2_gnn_in['b2'], 'L3_gnn_Wq': _L3_gnn_in['Wq'], 'L3_gnn_bq': _L3_gnn_in['bq'], 'L3_gnn_Wk': _L3_gnn_in['Wk'], 'L3_gnn_bk': _L3_gnn_in['bk'], 'L3_gnn_Wv': _L3_gnn_in['Wv'], 'L3_gnn_bv': _L3_gnn_in['bv'], 'L3_gnn_Wskip': _L3_gnn_in['Wskip'], 'L3_gnn_bskip': _L3_gnn_in['bskip']}

def reference(x, src, dst, edge_attr_128, edge_type_8, edge_weight, L0_gnn_g1, L0_gnn_b1, L0_gnn_g2, L0_gnn_b2, L0_gnn_eps_gin, L0_gnn_Wg1, L0_gnn_bg1, L0_gnn_Wg2, L0_gnn_bg2, L0_gnn_Wf1, L0_gnn_bf1, L0_gnn_Wf2, L0_gnn_bf2, L1_gnn_eps, L2_gnn_eps, L2_gnn_W1, L2_gnn_b1, L2_gnn_gamma, L2_gnn_beta, L2_gnn_W2, L2_gnn_b2, L3_gnn_Wq, L3_gnn_bq, L3_gnn_Wk, L3_gnn_bk, L3_gnn_Wv, L3_gnn_bv, L3_gnn_Wskip, L3_gnn_bskip):
    import jax
    import jax.numpy as jnp

    def _L0_gnn_ref(x, edge_index, edge_attr, g1, b1, g2, b2, eps_gin, Wg1, bg1, Wg2, bg2, Wf1, bf1, Wf2, bf2):
        import jax, jax.numpy as jnp
        import numpy as np
        N = 50000
        E = 625000
        D = 128
        DF = 4 * D

        def layernorm(x, gamma, beta, eps=1e-05):
            mu = jnp.mean(x, axis=-1, keepdims=True)
            var = jnp.var(x, axis=-1, keepdims=True)
            return (x - mu) * jax.lax.rsqrt(var + eps) * gamma + beta
        src = edge_index[0]
        dst = edge_index[1]
        xn = layernorm(x, g1, b1)
        msg = jax.nn.relu(xn[src] + edge_attr)
        aggr = jax.ops.segment_sum(msg, dst, num_segments=N)
        h = (1.0 + eps_gin) * xn + aggr
        h = jax.nn.relu(h @ Wg1 + bg1) @ Wg2 + bg2
        x = x + h
        xn2 = layernorm(x, g2, b2)
        f = jax.nn.gelu(xn2 @ Wf1 + bf1, approximate=False) @ Wf2 + bf2
        return x + f

    def _L1_gnn_ref(edge_index, X, num_nodes, eps):
        import jax, jax.numpy as jnp
        import numpy as np
        N_NODES = 20000
        N_EDGES = 10000
        D_FEAT = 128
        row = edge_index[0]
        col = edge_index[1]
        msgs = X[col]
        neigh = jax.ops.segment_sum(msgs, row, num_segments=num_nodes)
        rst = (1.0 + eps) * X + neigh
        return rst

    def _L2_gnn_ref(x, edge_index, eps, W1, b1, gamma, beta, W2, b2):
        import jax, jax.numpy as jnp
        import numpy as np
        N, E, D = (100000, 9375, 128)
        BN_EPS = 1e-05
        src, dst = (edge_index[0], edge_index[1])
        n = x.shape[0]
        agg = jax.ops.segment_sum(x[src], dst, num_segments=n)
        h = (1.0 + eps) * x + agg
        h = h @ W1.T + b1
        mean = jnp.mean(h, axis=0)
        var = jnp.mean(jnp.square(h - mean), axis=0)
        h = (h - mean) * jax.lax.rsqrt(var + BN_EPS) * gamma + beta
        h = jax.nn.relu(h)
        h = h @ W2.T + b2
        return x + jax.nn.relu(h)

    def _L3_gnn_ref(node_features, edge_index, edge_norm, edge_type, Wq, bq, Wk, bk, Wv, bv, Wskip, bskip):
        import jax, jax.numpy as jnp
        import numpy as np
        N = 50000
        E = 12500
        G = 128
        H = 128
        src = edge_index[0]
        dst = edge_index[1]
        q = node_features @ Wq + bq
        k = node_features @ Wk + bk
        v = node_features @ Wv + bv
        scale = jnp.asarray(1.0 / np.sqrt(H), node_features.dtype)
        logits = jnp.sum(q[dst] * k[src], axis=-1) * scale
        m = jax.ops.segment_max(logits, dst, num_segments=N)
        p = jnp.exp(logits - m[dst])
        denom = jax.ops.segment_sum(p, dst, num_segments=N)
        alpha = p / denom[dst]
        agg = jax.ops.segment_sum(alpha[:, None] * v[src], dst, num_segments=N)
        return agg + node_features @ Wskip + bskip
    edge_index = jnp.stack([src, dst])
    x = _layernorm(x + _L0_gnn_ref(x, edge_index, edge_attr_128, L0_gnn_g1, L0_gnn_b1, L0_gnn_g2, L0_gnn_b2, L0_gnn_eps_gin, L0_gnn_Wg1, L0_gnn_bg1, L0_gnn_Wg2, L0_gnn_bg2, L0_gnn_Wf1, L0_gnn_bf1, L0_gnn_Wf2, L0_gnn_bf2), axis=-1)
    x = _layernorm(x + _L1_gnn_ref(edge_index, x, 50000, L1_gnn_eps), axis=-1)
    x = _layernorm(x + _L2_gnn_ref(x, edge_index, L2_gnn_eps, L2_gnn_W1, L2_gnn_b1, L2_gnn_gamma, L2_gnn_beta, L2_gnn_W2, L2_gnn_b2), axis=-1)
    x = _layernorm(x + _L3_gnn_ref(x, edge_index, edge_weight, edge_type_8, L3_gnn_Wq, L3_gnn_bq, L3_gnn_Wk, L3_gnn_bk, L3_gnn_Wv, L3_gnn_bv, L3_gnn_Wskip, L3_gnn_bskip), axis=-1)
    return x

_drawn_inputs = setup_inputs


def setup_inputs(seed=0):
    import zlib

    import numpy as np

    out = dict(_drawn_inputs(seed))
    spreads = {'L0_gnn_g1': (1.0, 0.584),
     'L0_gnn_b1': (0.0, 0.57),
     'L0_gnn_g2': (1.0, 0.6),
     'L0_gnn_b2': (0.0, 0.78),
     'L0_gnn_bg1': (0.0, 0.382),
     'L0_gnn_bg2': (0.0, 0.1),
     'L0_gnn_bf1': (0.0, 0.403),
     'L0_gnn_bf2': (0.0, 0.1),
     'L2_gnn_gamma': (1.0, 0.6),
     'L2_gnn_beta': (0.0, 0.535)}
    factors = {'L2_gnn_b1': 200.0,
     'L2_gnn_b2': 2.727,
     'L3_gnn_bq': 198.822,
     'L3_gnn_bk': 200.0,
     'L3_gnn_bv': 8.0,
     'L3_gnn_bskip': 7.585}
    for name, (base, spread) in spreads.items():
        noise = np.random.default_rng([zlib.crc32(name.encode()), seed]).standard_normal(out[name].shape)
        drawn = base * np.exp(spread * noise) if base else spread * noise
        out[name] = jnp.asarray(drawn.astype(out[name].dtype))
    for name, factor in factors.items():
        out[name] = (out[name] * factor).astype(out[name].dtype)
    return out
```

```python
from contextlib import ExitStack

import concourse.bass as bass
from concourse import mybir

F32 = mybir.dt.float32
I32 = mybir.dt.int32
U8 = mybir.dt.uint8
ALU = mybir.AluOpType
ACT = mybir.ActivationFunctionType

P = 128
N = 50000
E = 12500
D = 128
DF = 4 * D
R = 4
G = P * R
NG = -(-N // G)
LAST = N - G
SEEN = (NG - 1) * G - LAST
EG = 25
EP = EG * G
ET = EG * R
FAR = 65536
LN_EPS = 1e-5
BN_EPS = 1e-5
SM_SCALE = float(D) ** -0.5
BIG = 1e30
MAP_P = 80
PC = 5
KC = 20
KW = EP // KC
PIPE = NG + EG
MAP_PUT, MAP_GET, PRE_GOT = 2, 12, 24
MAP_PAIRS = ET // PC // 2


class Group:

    def __init__(self, i, b, kind):
        self.i, self.b, self.kind = i, b, kind
        self.g = 2 * i + b
        self.n = self.g + 1
        self.j = self.g - NG


def node_row(q):
    if isinstance(q.i, int) and q.g == NG - 1:
        return LAST
    return q.g * G


def build(nc, a):
    ctx = ExitStack()
    with ctx:
        def sb(name, shape, dt=F32):
            return ctx.enter_context(nc.sbuf_tensor(name, shape, dt))

        def pb(name, shape=(P, G)):
            return ctx.enter_context(nc.psum_tensor(name, list(shape), F32))

        def sem(name):
            return ctx.enter_context(nc.semaphore(name))

        def pair(name):
            return [sem(name + "0"), sem(name + "1")]

        def f(t):
            return t.rearrange("p r d -> p (r d)")

        xA = nc.dram_tensor("table_a", (N + EP, D), F32).ap()
        Y = nc.dram_tensor("table_y", (N + G, D), F32).ap()
        xB = nc.dram_tensor("table_b", (N, D), F32).ap()
        xC = nc.dram_tensor("table_c", (N + EP, D), F32).ap()
        newest = nc.dram_tensor("newest", (N, 1), I32).ap()
        dst_tab = nc.dram_tensor("dst_sorted", (EP + 2,), I32).ap()
        src_tab = nc.dram_tensor("src_sorted", (EP,), I32).ap()
        perm_tab = nc.dram_tensor("edge_order", (EP,), I32).ap()

        ident = sb("ident", [P, P])
        ones = sb("ones", [P, P])
        mhalf = sb("mhalf", [P, 12])
        fresh = sb("fresh", [P, 1])
        Wg1, Wg2 = sb("Wg1", [P, D]), sb("Wg2", [P, D])
        Wf1, Wf2 = sb("Wf1", [P, DF]), sb("Wf2", [P, 4, D])
        Wq, Wk, Wv, Ws = sb("Wq", [P, D]), sb("Wk", [P, D]), sb("Wv", [P, D]), sb("Wskip", [P, D])
        W1, W2 = sb("W1", [P, D]), sb("W2", [P, D])
        W1T, W2T = sb("W1T", [P, D]), sb("W2T", [P, D])
        bg2r, bf2r, b2r, bsr = sb("bg2r", [P, D]), sb("bf2r", [P, D]), sb("b2r", [P, D]), sb("bsr", [P, D])
        COLS = ["g1", "b1", "g2", "b2", "bg1", "L2b1", "gamma", "beta", "bq", "bk", "bv"]
        cols = sb("cols", [P, len(COLS)])
        col = {n: cols[:, k:k + 1] for k, n in enumerate(COLS)}
        bf1c = sb("bf1c", [P, 4])
        eps3 = sb("eps3", [P, 3])
        k1 = sb("k1", [P, 6])
        one_eg, g1s, b1s, two_e1, two_e1sq, one_e2 = (k1[:, k:k + 1] for k in range(6))
        rows_i = sb("rows_i", [ET, 4, P], I32)
        rows_f = sb("rows_f", [ET, 8, P])
        skip_or_dst = sb("skip_or_dst", [P, ET], I32)
        dst_i = sb("dst_i", [P, ET], I32)
        src_i = sb("src_i", [P, ET], I32)
        perm_i = sb("perm_i", [P, ET], I32)
        pos_i = sb("pos_i", [P, ET], I32)
        news_i = sb("news_i", [P, ET], I32)
        newd_i = sb("newd_i", [P, ET], I32)
        src_f = sb("src_f", [P, ET])
        spare = sb("spare", [P, R])
        open_rows = sb("open_rows", [P, NG, R])
        is_last = sb("is_last", [P, ET])
        keep = sb("keep", [P, EP], U8)
        ixr = sb("ixr", [P, 2, 8], I32)
        ixs = sb("ixs", [P, 2, 8], I32)
        newr = sb("newr", [P, 2, 16], I32)
        X = sb("X", [P, ET, D])
        H = sb("H", [P, ET, D])
        HT = H[:].rearrange("p t d -> p (t d)")
        xin = sb("xin", [P, 2, R, D])
        gr = sb("gr", [P, 2, R, D])
        at = sb("at", [P, 2, R, D])
        w = {n: sb("w_" + n, [P, R, D]) for n in ("xh1", "h", "r", "xb", "xc", "x1", "xh2", "n2",
                                                  "xhs", "hraw", "ms", "ma", "msg", "f0", "f1")}
        gm = sb("gm", [P, R, D + 1])
        s2b = sb("s2b", [P, 2, R, D])
        gT = sb("gT", [P, 4, G])
        ub = sb("ub", [P, 2, R, D])
        oA = sb("oA", [P, 2, R, D])
        oB = sb("oB", [P, 2, R, D])
        stt = sb("stt", [P, 4, R, 6])
        mv = sb("mv", [P, 4, R, 2])
        vinc, vin2, vin3 = sb("vinc", [P, 12]), sb("vin2", [P, R]), sb("vin3", [P, R])
        nma, nmb, rb = sb("nma", [P, R]), sb("nmb", [P, R]), sb("rb", [P, R])
        mbig = sb("mbig", [P, 1])
        zero_row = sb("zero_row", [P, D + 1])
        order_rows = sb("order_rows", [ET, P], I32)
        ro = sb("ro", [P, 12])
        r2 = sb("r2", [P, R])
        r3 = sb("r3", [P, 2, R])
        sm = sb("sm", [P, 8, R])
        carry = sb("carry", [P, 4])
        keys = at[:].rearrange("p b r d -> p b (r d)").bitcast(I32)
        put_at = sb("put_at", [P, 2, R], I32)
        sums_at = sb("sums_at", [P, 2, R], I32)
        spare_i = sb("spare_i", [P, R], I32)
        cov = sb("cov", [P, D + 1])
        covE = sb("covE", [P, D + 1])
        bn = sb("bn", [P, 12])
        bn_a, bn_b = bn[:, 9:10], bn[:, 10:11]
        later_mask = HT[:, 0:R * G].rearrange("p (r g) -> p r g", r=R)
        l1_junk = [t[:, b].rearrange("p r d -> p (r d)") for t in (oB, ub) for b in range(2)]
        open_i = f(w["xhs"][:]).bitcast(I32)[:, 0:NG * R].rearrange("p (g r) -> p g r", g=NG)
        own_row = HT[0:MAP_P, 0:N // MAP_P].bitcast(I32)
        dstb = [t.bitcast(I32)[:, 0:KW + 1] for t in (gT[:, 0:2, :].rearrange("p c g -> p (c g)"), gT[:, 2:4, :].rearrange("p c g -> p (c g)"))]
        pT1, pT2, pm1, pm2, pm4, pG = (pb(x) for x in ("pT1", "pT2", "pm1", "pm2", "pm4", "pG"))
        pm3 = [pb("pm3a"), pb("pm3b")]

        def rows4(ap):
            return ap.rearrange("(p r) d -> p r d", r=R)

        def store_rows(sp, table, q, buf):
            if isinstance(q.i, int) and q.g == NG - 1:
                return sp.dma_start(rows4(table[LAST + SEEN:N, :]), buf[SEEN // R:P])
            return sp.dma_start(rows4(table[span(q.g * G, G), :]), buf)

        def edge4(ap):
            return ap.rearrange("(r p) d -> p r d", p=P)

        def span(start, size):
            return slice(start, start + size) if isinstance(start, int) else bass.ds(start, size)

        def ge(eng, s, v):
            if not (isinstance(v, int) and v <= 0):
                eng.wait_ge(s, v)

        def after_wait(eng):
            eng.sem_inc(waited, 1)

        def bcast(t):
            return t[:].unsqueeze(1).to_broadcast([P, R, D])

        const_loaded = sem("const_loaded")
        waited = sem("waited")
        pool_const = sem("pool_const")
        tables_written = sem("tables_written")
        rows_loaded = sem("rows_loaded")
        setup_dve = sem("setup_dve")
        setup_pe = sem("setup_pe")
        idx_ready = sem("idx_ready")
        dstb_loaded = pair("dstb_loaded")
        keep_made = sem("keep_made")

        def const_dmas():
            for t, k in ((Wg1, "L0_gnn_Wg1"), (Wg2, "L0_gnn_Wg2"), (Wf1, "L0_gnn_Wf1"), (Wq, "L3_gnn_Wq"),
                         (Wk, "L3_gnn_Wk"), (Wv, "L3_gnn_Wv"), (Ws, "L3_gnn_Wskip"), (W1, "L2_gnn_W1"),
                         (W2, "L2_gnn_W2")):
                yield t[:], a[k]
            yield Wf2[:], a["L0_gnn_Wf2"].rearrange("(c p) d -> p c d", p=P)
            for c in range(4):
                yield bf1c[:, c:c + 1], a["L0_gnn_bf1"][c * P:(c + 1) * P].rearrange("(p o) -> p o", o=1)
            for n, k in zip(COLS, ("L0_gnn_g1", "L0_gnn_b1", "L0_gnn_g2", "L0_gnn_b2", "L0_gnn_bg1",
                                   "L2_gnn_b1", "L2_gnn_gamma", "L2_gnn_beta", "L3_gnn_bq", "L3_gnn_bk",
                                   "L3_gnn_bv")):
                yield col[n], a[k].rearrange("(p o) -> p o", o=1)
            for t, k in ((bg2r, "L0_gnn_bg2"), (bf2r, "L0_gnn_bf2"), (b2r, "L2_gnn_b2"), (bsr, "L3_gnn_bskip")):
                yield t[:], a[k].partition_broadcast(P)
            for c, k in enumerate(("L0_gnn_eps_gin", "L1_gnn_eps", "L2_gnn_eps")):
                yield eps3[:, c:c + 1], a[k].partition_broadcast(P)

        CONST = 16 * len(list(const_dmas()))
        POOL_CONST, ROWS_READY, SETUP_DVE, IDX_READY = 15, 17, 25, 1
        BN_COV, BN_QUAD, BN_VAR, BN_DONE = 5, 7, 11, 1

        def run_pipeline(fori, step):
            def peeled(first, end):
                for s in range(first, end):
                    at_stage = [Group((s - lag) // 2, (s - lag) % 2, "N" if s - lag < NG else "E")
                                if 0 <= s - lag < PIPE else None for lag in range(5)]
                    step(s // 2, s % 2, *at_stage)

            def looped(first, end, kind, work=None):
                with fori(first, end) as i:
                    for k in range(2):
                        step(i, k, *(Group(i + (k - lag) // 2, (k - lag) % 2, kind) for lag in range(5)),
                             work=work)

            peeled(0, 2 * MAP_PUT)
            looped(MAP_PUT, MAP_GET, "N", "put")
            looped(MAP_GET, MAP_GET + MAP_PAIRS, "N", "get")
            looped(MAP_GET + MAP_PAIRS, PRE_GOT, "N")
            looped(PRE_GOT, NG // 2 - 1, "N", "pre")
            for s in (NG - 2, NG - 1):
                step(s // 2, s % 2, *(Group((s - lag) // 2, (s - lag) % 2, "N") for lag in range(5)), work="pre")
            peeled(NG, NG + 4)
            looped((NG + 4) // 2, (PIPE - 1) // 2, "E")
            peeled(PIPE - 1, PIPE + 4)

        def edge_groups(fori, step, lag=0):
            step(Group(0, 0, "E"), None)
            step(Group(0, 1, "E"), Group(0, 0, "E"))
            with fori(1, EG // 2) as i:
                step(Group(i, 0, "E"), Group(i - 1, 1, "E"))
                step(Group(i, 1, "E"), Group(i, 0, "E"))
            step(Group(EG // 2, 0, "E"), Group(EG // 2 - 1, 1, "E"))
            step(None, Group(EG // 2, 0, "E"))

        def node_groups(fori, step):
            step(Group(0, 0, "N"), None)
            step(Group(0, 1, "N"), Group(0, 0, "N"))
            with fori(1, NG // 2 - 1) as i:
                step(Group(i, 0, "N"), Group(i - 1, 1, "N"))
                step(Group(i, 1, "N"), Group(i, 0, "N"))
            for g in (NG - 2, NG - 1):
                step(Group(g // 2, g % 2, "N"), Group((g - 1) // 2, (g - 1) % 2, "N"))
            step(None, Group((NG - 1) // 2, (NG - 1) % 2, "N"))

        def tile(ap, q, r):
            return ap[:, span(q * R + r, 1), :].rearrange("p o d -> p (o d)")

        x_loaded = pair("x_loaded")
        attr_got = pair("attr_got")
        var = {n: sem("var_" + n) for n in "123s"}
        nma_made, nmb_made = sem("nma_made"), sem("nmb_made")
        powc, pow2, pow3 = sem("powc"), sem("pow2"), sem("pow3")
        xb_made, xc_made, s_made = sem("xb_made"), sem("xc_made"), sem("s_made")
        xh1_made, xh2_made, xhs_made = sem("xh1_made"), sem("xh2_made"), sem("xhs_made")
        x1_made, u_made = sem("x1_made"), sem("u_made")
        t1_done, t2_done, ts_done, ta_done = sem("t1_done"), sem("t2_done"), sem("ts_done"), sem("ta_done")
        h_made, hraw_made, he_made, n2_made = sem("h_made"), sem("hraw_made"), sem("he_made"), sem("n2_made")
        mm1_done, mm2_done, mm3_done, mm4_done = sem("mm1_done"), sem("mm2_done"), sem("mm3_done"), sem("mm4_done")
        r_made, gelu_made = sem("r_made"), sem("gelu_made")
        xA_made, y_made = sem("xA_made"), sem("y_made")
        xA_stored, y_stored = pair("xA_stored"), pair("y_stored")
        later_made = sem("later_made")
        y_put, spare_zero, open_loaded = pair("y_put"), sem("spare_zero"), sem("open_loaded")
        xAe_stored = pair("xAe_stored")
        ms_made, ma_made, msg_made, agg_made = sem("ms_made"), sem("ma_made"), sem("msg_made"), sem("agg_made")
        map_put, map_got, new_kept = pair("map_put"), pair("map_got"), pair("new_kept")
        ix_put, ix_got, ix_pre, ix_attr, ix_old = sem("ix_put"), sem("ix_got"), sem("ix_pre"), sem("ix_attr"), sem("ix_old")
        pre_got, pre_kept = pair("pre_got"), pair("pre_kept")

        class Steps:

            def __init__(self, prefix, *chains):
                self.where = {}
                for chain in chains:
                    names = chain.split()
                    s = sem(prefix + names[0])
                    for k, name in enumerate(names):
                        self.where[name] = s, k + 1, len(names)

            def __getitem__(self, name):
                return self.where[name][0]

            def at(self, name, n):
                _, k, total = self.where[name]
                return total * (n - 1) + k if total > 1 else n

        l1 = Steps("l1_", "ix", "same count far dup away mul idx", "sum", "rows")
        l1_got, l1_added, l1_keys = pair("l1_got"), pair("l1_added"), pair("l1_keys")
        nb = Steps("nb_", "var", "pw", "x", "m", "gram")
        nb_loaded, nb_stored = pair("nb_loaded"), pair("nb_stored")
        l2 = Steps("l2_", "ix", "t tb", "tg gram mm", "scan g", "gm gt h", "x")
        l2_got, l2_own = pair("l2_got"), pair("l2_own")
        bns = Steps("bn_", "open", "dve", "pe", "pw", "ready")
        q2 = Steps("q2_", "r rt", "mm", "t y", "var", "pw", "x")
        q2_stored = pair("q2_stored")
        n2 = Steps("n2_", "ta mm1 mm2", "tc mm3", "c r rt", "ct o", "t y xc", "z nm", "var", "var2",
                   "xcb", "pw", "pw2")
        n2_loaded, n2_cst, n2_ost = pair("n2_loaded"), pair("n2_cst"), pair("n2_ost")
        l3 = Steps("l3_", "ix", "ts td mq mk mv ml mm", "xs xd q pen l c p",
                   "qk m carry e1 e2 lm num nsc den rc o xb z", "var", "pw", "out")
        l3_got, l3_own, l3_put, l3_ix_put = pair("l3_got"), pair("l3_own"), pair("l3_put"), sem("l3_ix_put")

        PAIRS_N = NG // 2

        block = ctx.enter_context(nc.Block())

        @block.sync
        def _(sp):
            for dst, src in const_dmas():
                sp.dma_start(dst, src).then_inc(const_loaded, 16)
            sp.wait_ge(pool_const, POOL_CONST)
            pad, zero = rows_i[0:1, 0:3, :].rearrange("a b c -> a (b c)"), rows_i[0:1, 3, :]
            sp.dma_start(dst_tab[0:1].unsqueeze(0), pad[:, 0:1]).then_inc(tables_written, 16)
            sp.dma_start(dst_tab[1:1 + E], a["dst"]).then_inc(tables_written, 16)
            sp.dma_start(dst_tab[1 + E:EP + 2].unsqueeze(0), pad[:, 0:EP + 1 - E]).then_inc(tables_written, 16)
            sp.dma_start(src_tab[0:E], a["src"]).then_inc(tables_written, 16)
            for c in range(3):
                sp.dma_start(src_tab[E + 100 * c:E + 100 * (c + 1)].unsqueeze(0),
                             zero[:, 0:100]).then_inc(tables_written, 16)
            sp.dma_start(perm_tab.rearrange("(t p) -> t p", p=P), order_rows[:]).then_inc(tables_written, 16)
            sp.dma_start(newest.rearrange("(p r) o -> p (r o)", p=MAP_P), own_row).then_inc(tables_written, 16)
            sp.wait_ge(tables_written, 16 * 9)
            sp.dma_start(edge4(Y[N:N + G, :]), oB[:, 0]).then_inc(spare_zero, 16)
            for k, t in enumerate((dst_tab[1:1 + EP], dst_tab[2:2 + EP], src_tab, perm_tab)):
                sp.dma_start(rows_i[:, k, :], t.rearrange("(t p) -> t p", p=P)).then_inc(rows_loaded, 16)
            for c in range(KC):
                ge(sp, keep_made, c - 1)
                sp.dma_start(dstb[c % 2], dst_tab[c * KW:c * KW + KW + 1].partition_broadcast(P)).then_inc(dstb_loaded[c % 2], 16)

            def load(q):
                ge(sp, xh1_made, q.n - 2)
                ge(sp, xb_made, q.n - 2)
                ge(sp, xc_made, q.n - 2)
                sp.dma_start(xin[:, q.b], rows4(a["x"][span(node_row(q), G), :])).then_inc(x_loaded[q.b], 16)

            def step(i, k, fr, mi, ba, ta, od, work=None):
                if fr is not None and fr.kind == "N" and not (isinstance(fr.i, int) and fr.g == NG - 1):
                    load(Group(fr.i + (fr.b + 1) // 2, 1 - fr.b, "N"))
                if ta is not None:
                    sp.wait_ge(xA_made, ta.n)
                    if ta.kind == "N":
                        store_rows(sp, xA, ta, oA[:, ta.b]).then_inc(xA_stored[ta.b], 16)
                        sp.wait_ge(y_made, ta.n)
                        store_rows(sp, Y, ta, oB[:, ta.b]).then_inc(y_stored[ta.b], 16)
                    else:
                        sp.dma_start(edge4(xA[span(N + ta.j * G, G), :]), X[:, span(ta.j * R, R), :]).then_inc(xAe_stored[ta.b], 16)
                if work == "get":
                    c = 2 * (i - MAP_GET) + k
                    sp.wait_ge(map_got[k], 32 * PC * (i - MAP_GET + 1))
                    sp.dma_start(news_i[:, span(c * PC, PC)], newr[:, k, 0:PC]).then_inc(new_kept[k], 16)
                    sp.dma_start(newd_i[:, span(c * PC, PC)], newr[:, k, 8:8 + PC]).then_inc(new_kept[k], 16)
                if work == "pre":
                    sp.wait_ge(pre_got[k], 16 * R * (i - PRE_GOT + 1))
                    after_wait(sp)
                    sp.dma_start((X if k else H)[:, span((i - PRE_GOT) * R, R), :], gr[:, k]).then_inc(pre_kept[k], 16)

            load(Group(0, 0, "N"))
            run_pipeline(nc.sync.Fori, step)

            sp.wait_ge(ts_done, EG)
            for b in range(2):
                sp.wait_ge(map_put[b], 16 * PC * MAP_PAIRS)
            for g in range(NG):
                row = LAST if g == NG - 1 else g * G
                sp.dma_start(open_i[:, g, :], newest[row:row + G, :].rearrange("(p r) o -> p (r o)", r=R)).then_inc(open_loaded, 16)

            def l1_step(q, _):
                if q is not None:
                    ge(sp, l1["same"], l1.at("same", q.n - 2))
                    sp.dma_start(keys[:, q.b], src_tab[span(q.g * G, G)].partition_broadcast(P)).then_inc(l1_keys[q.b], 16)
            edge_groups(nc.sync.Fori, l1_step)

            for b in range(2):
                sp.wait_ge(l1_added[b], 16 * R * ((EG + 1 - b) // 2))

            def nb_load(p):
                ge(sp, nb["x"], nb.at("x", p.n - 2))
                after_wait(sp)
                sp.dma_start(xin[:, p.b], rows4(Y[span(node_row(p), G), :])).then_inc(nb_loaded[p.b], 16)

            def nb_step(p, before):
                if p is not None and not (isinstance(p.i, int) and p.g == NG - 1):
                    nb_load(Group(p.i + (p.b + 1) // 2, 1 - p.b, "N"))
                if before is not None:
                    sp.wait_ge(nb["x"], nb.at("x", before.n))
                    store_rows(sp, xB, before, oA[:, before.b]).then_inc(nb_stored[before.b], 16)
            nb_load(Group(0, 0, "N"))
            node_groups(nc.sync.Fori, nb_step)

            def q2_store(q, _):
                if q is not None:
                    sp.wait_ge(q2["x"], q2.at("x", q.n))
                    sp.dma_start(edge4(xC[span(N + q.g * G, G), :]), X[:, span(q.g * R, R), :]).then_inc(q2_stored[q.b], 16)
            edge_groups(nc.sync.Fori, q2_store)

            def n2_load(p):
                ge(sp, n2["ta"], n2.at("ta", p.n - 2))
                after_wait(sp)
                ge(sp, n2["y"], n2.at("y", p.n - 2))
                after_wait(sp)
                sp.dma_start(xin[:, p.b], rows4(xB[span(node_row(p), G), :])).then_inc(n2_loaded[p.b], 16)

            def n2_step(p, before):
                if p is not None and not (isinstance(p.i, int) and p.g == NG - 1):
                    n2_load(Group(p.i + (p.b + 1) // 2, 1 - p.b, "N"))
                if p is not None:
                    sp.wait_ge(n2["xc"], n2.at("xc", p.n))
                    store_rows(sp, xC, p, oA[:, p.b]).then_inc(n2_cst[p.b], 16)
                if before is not None:
                    sp.wait_ge(n2["o"], n2.at("o", before.n))
                    store_rows(sp, a["out"], before, s2b[:, before.b]).then_inc(n2_ost[before.b], 16)
            n2_load(Group(0, 0, "N"))
            node_groups(nc.sync.Fori, n2_step)
            for b in range(2):
                sp.wait_ge(n2_ost[b], 16 * PAIRS_N)
                sp.wait_ge(l3_put[b], 16 * R * ((EG + 1 - b) // 2))

        @block.gpsimd
        def _(pool):
            POOL = nc.gpsimd
            POOL.memset(gm[:], 0.0).then_inc(pool_const, 1)
            POOL.memset(ident[:], 0.0).then_inc(pool_const, 1)
            POOL.memset(ones[:], 1.0).then_inc(pool_const, 1)
            POOL.memset(mhalf[:], -0.5).then_inc(pool_const, 1)
            POOL.memset(vinc[:], 1.0).then_inc(pool_const, 1)
            POOL.memset(oB[:], 0.0).then_inc(pool_const, 1)
            POOL.iota(spare_i[:], [[P, R]], base=N, channel_multiplier=1).then_inc(pool_const, 1)
            POOL.memset(rows_i[:, 0:3, :], FAR - 1).then_inc(pool_const, 1)
            POOL.memset(rows_i[:, 3, :], FAR - 1).then_inc(pool_const, 1)
            POOL.memset(fresh[:], 1.0).then_inc(pool_const, 1)
            POOL.iota(order_rows[:], [[1, P]], base=0, channel_multiplier=P).then_inc(pool_const, 1)
            POOL.iota(own_row, [[1, N // MAP_P]], base=0, channel_multiplier=N // MAP_P).then_inc(pool_const, 1)
            POOL.iota(pos_i[:], [[P, ET]], base=N, channel_multiplier=1).then_inc(pool_const, 1)
            pool.wait_ge(pool_const, 13)
            POOL.affine_select(out=ident[:], in_=ident[:], compare_op=ALU.not_equal, fill=1.0, base=0,
                               pattern=[[-1, P]], channel_multiplier=1).then_inc(pool_const, 1)
            POOL.affine_select(out=fresh[:], in_=fresh[:], compare_op=ALU.is_ge, fill=0.0, base=-(SEEN // R),
                               pattern=[[0, 1]], channel_multiplier=1).then_inc(pool_const, 1)
            pool.wait_ge(const_loaded, CONST)
            pool.wait_ge(idx_ready, IDX_READY)

            def inverse_root(out, in_):
                return POOL.tensor_tensor(out, in_, mhalf[:, 0:in_.shape[-1]], ALU.pow)

            def gather(dst, table, index, s):
                POOL.indirect_dma_start(dst, None, table, bass.IndirectOffsetOnAxis(ap=index, axis=0)).then_inc(s, 16)

            def indices(ring, lst, t, count, s, n):
                POOL.tensor_copy(ring[:, 0:count], lst[:, span(t, count)]).then_inc(s, 1)
                pool.wait_ge(s, n)
                after_wait(pool)

            def attr_gather(j, i, b):
                ge(pool, ta_done, j - 1)
                indices(ixr[:, b], perm_i, j * R, R, ix_attr, j + 1)
                for r in range(R):
                    gather(at[:, b, r, :], a["edge_attr_128"], ixr[:, b, r:r + 1], attr_got[b])

            def step(i, k, fr, mi, ba, ta, od, work=None):
                if fr is not None:
                    pool.wait_ge(var["1"], 3 * fr.n)
                    if fr.kind == "E":
                        pool.wait_ge(var["s"], 3 * (fr.j + 1))
                        ge(pool, xhs_made, fr.j)
                    ge(pool, xh1_made, fr.n - 1)
                    inverse_root(ro[:], vinc[:]).then_inc(powc, 1)
                if work == "put":
                    c = 2 * (i - MAP_PUT) + k
                    ge(pool, map_put[k], 16 * PC * (i - MAP_PUT))
                    indices(ixr[:, k], skip_or_dst, c * PC, PC, ix_put, 2 * c + 1)
                    indices(ixs[:, k], pos_i, c * PC, PC, ix_put, 2 * c + 2)
                    for t in range(PC):
                        POOL.indirect_dma_start(newest, bass.IndirectOffsetOnAxis(ap=ixr[:, k, t:t + 1], axis=0),
                                                ixs[:, k, t:t + 1], None, bounds_check=N - 1,
                                                oob_is_err=False).then_inc(map_put[k], 16)
                if work == "get":
                    c = 2 * (i - MAP_GET) + k
                    for b in range(2):
                        pool.wait_ge(map_put[b], 16 * PC * MAP_PAIRS)
                    ge(pool, new_kept[k], 32 * (i - MAP_GET))
                    indices(ixr[:, k], src_i, c * PC, PC, ix_got, c + 1)
                    indices(ixs[:, k], dst_i, c * PC, PC, ix_old, c + 1)
                    for t in range(PC):
                        gather(newr[:, k, t:t + 1], newest, ixr[:, k, t:t + 1], map_got[k])
                        gather(newr[:, k, 8 + t:9 + t], newest, ixs[:, k, t:t + 1], map_got[k])
                if work == "pre":
                    ge(pool, pre_kept[k], 16 * (i - PRE_GOT))
                    indices(ixr[:, k], dst_i if k else src_i, (i - PRE_GOT) * R, R, ix_pre, 2 * (i - PRE_GOT) + k + 1)
                    for r in range(R):
                        gather(gr[:, k, r, :], a["x"], ixr[:, k, r:r + 1], pre_got[k])
                if fr is not None and fr.kind == "E":
                    if isinstance(fr.i, int) and fr.j == 0:
                        attr_gather(0, NG // 2, 0)
                    if not (isinstance(fr.i, int) and fr.j == EG - 1):
                        attr_gather(fr.j + 1, fr.i + (fr.b + 1) // 2, 1 - fr.b)
                if mi is not None:
                    pool.wait_ge(var["2"], 3 * mi.n)
                    ge(pool, xh2_made, mi.n - 1)
                    inverse_root(r2[:], vin2[:]).then_inc(pow2, 1)
                    pool.wait_ge(x1_made, mi.n)
                    pool.wait_ge(xc_made, mi.n)
                    ge(pool, u_made, mi.n - 2)
                    POOL.tensor_tensor(s2b[:, mi.b], w["xc"][:], w["x1"][:], ALU.add).then_inc(s_made, 1)
                if fr is not None:
                    ge(pool, s_made, fr.n - 1)
                    if fr.kind == "N":
                        pool.wait_ge(x_loaded[fr.b], 16 * (fr.i + 1))
                        x = xin[:, fr.b]
                    else:
                        pool.wait_ge(pre_kept[1], 16 * EG)
                        x = X[:, span(fr.j * R, R), :]
                    POOL.tensor_tensor(w["xc"][:], x, bcast(bf2r), ALU.add).then_inc(xc_made, 1)
                if ta is not None and ta.kind == "E":
                    for b in range(2):
                        pool.wait_ge(y_stored[b], 16 * PAIRS_N)
                    ge(pool, y_put[ta.b], 16 * R * (ta.i - NG // 2))
                    indices(ixs[:, ta.b], skip_or_dst, ta.j * R, R, ix_put, 2 * 2 * MAP_PAIRS + ta.j + 1)
                    pool.wait_ge(y_made, ta.n)
                    after_wait(pool)
                    for r in range(R):
                        POOL.indirect_dma_start(Y, bass.IndirectOffsetOnAxis(ap=ixs[:, ta.b, r:r + 1], axis=0),
                                                oB[:, ta.b, r, :], None, bounds_check=N - 1,
                                                oob_is_err=False).then_inc(y_put[ta.b], 16)
                if ba is not None:
                    pool.wait_ge(var["3"], 3 * ba.n)
                    ge(pool, xA_made, ba.n - 2)
                    ge(pool, y_made, ba.n - 2)
                    inverse_root(r3[:, ba.b], vin3[:]).then_inc(pow3, 1)

            run_pipeline(POOL.Fori, step)

            pool.wait_ge(xhs_made, EG)
            POOL.memset(later_mask, 1.0).then_inc(later_made, 1)
            pool.wait_ge(later_made, 1)
            POOL.affine_select(out=later_mask, in_=later_mask, compare_op=ALU.is_gt, fill=0.0, base=0,
                               pattern=[[-P, R], [1, G]], channel_multiplier=-1).then_inc(later_made, 1)
            pool.wait_ge(spare_zero, 16)
            for b in range(2):
                pool.wait_ge(xA_stored[b], 16 * PAIRS_N)
                pool.wait_ge(xAe_stored[b], 16 * ((EG + 1 - b) // 2))
                pool.wait_ge(new_kept[b], 32 * MAP_PAIRS)
                pool.wait_ge(y_put[b], 16 * R * ((EG + 1 - b) // 2))

            def l1_step(q, before):
                if q is not None:
                    ge(pool, l1["sum"], l1.at("sum", q.n - 2))
                    indices(ixr[:, q.b], newd_i, q.g * R, R, l1["ix"], q.n)
                    for r in range(R):
                        gather(gr[:, q.b, r, :], xA, ixr[:, q.b, r:r + 1], l1_got[q.b])
                if before is not None:
                    pool.wait_ge(l1["idx"], l1.at("idx", before.n))
                    pool.wait_ge(l1["rows"], l1.at("rows", before.n))
                    ge(pool, l1_added[1 - before.b], 16 * R * (before.i + before.b))
                    after_wait(pool)
                    for r in range(R):
                        POOL.indirect_dma_start(Y, bass.IndirectOffsetOnAxis(ap=sums_at[:, before.b, r:r + 1], axis=0),
                                                oA[:, before.b, r, :], None, bounds_check=N + G - 1,
                                                compute_op=ALU.add).then_inc(l1_added[before.b], 16)
            edge_groups(POOL.Fori, l1_step)

            def nb_step(p, before):
                if p is not None:
                    pool.wait_ge(nb["var"], 3 * p.n)
                    ge(pool, nb["x"], nb.at("x", p.n - 1))
                    inverse_root(r2[:], vin2[:]).then_inc(nb["pw"], 1)
            node_groups(POOL.Fori, nb_step)

            for b in range(2):
                pool.wait_ge(nb_stored[b], 16 * PAIRS_N)

            def l2_step(q, before):
                if q is not None:
                    ge(pool, l2["t"], l2.at("t", q.n - 2))
                    ge(pool, l2["g"], l2.at("g", q.n - 2))
                    ge(pool, l2["x"], l2.at("x", q.n - 2))
                    indices(ixr[:, q.b], src_i, q.g * R, R, l2["ix"], 2 * q.g + 1)
                    indices(ixs[:, q.b], dst_i, q.g * R, R, l2["ix"], 2 * q.g + 2)
                    for r in range(R):
                        gather(gr[:, q.b, r, :], xB, ixr[:, q.b, r:r + 1], l2_got[q.b])
                        gather(at[:, q.b, r, :], xB, ixs[:, q.b, r:r + 1], l2_own[q.b])
            edge_groups(POOL.Fori, l2_step)
            pool.wait_ge(bns["dve"], BN_VAR)
            inverse_root(bn[:, 5:6], bn[:, 4:5]).then_inc(bns["pw"], 1)

            def q2_step(q, before):
                if q is not None:
                    pool.wait_ge(q2["var"], 3 * q.n)
                    ge(pool, q2["x"], q2.at("x", q.n - 1))
                    inverse_root(r2[:], vin2[:]).then_inc(q2["pw"], 1)
            edge_groups(POOL.Fori, q2_step)

            def n2_step(p, before):
                if p is not None:
                    pool.wait_ge(n2["var"], 3 * p.n)
                    ge(pool, n2["xc"], n2.at("xc", p.n - 1))
                    inverse_root(r2[:], vin2[:]).then_inc(n2["pw"], 1)
                if before is not None:
                    pool.wait_ge(n2["var2"], 3 * before.n)
                    ge(pool, n2["o"], n2.at("o", before.n - 2))
                    inverse_root(r3[:, before.b], vin3[:]).then_inc(n2["pw2"], 1)
                if p is not None:
                    pool.wait_ge(n2["xc"], n2.at("xc", p.n))
                    ge(pool, n2["z"], n2.at("z", p.n - 1))
                    POOL.tensor_tensor(w["xb"][:], oA[:, p.b], bcast(bsr), ALU.add).then_inc(n2["xcb"], 1)
            node_groups(POOL.Fori, n2_step)

            for b in range(2):
                pool.wait_ge(n2_cst[b], 16 * PAIRS_N)
                pool.wait_ge(q2_stored[b], 16 * ((EG + 1 - b) // 2))
                pool.wait_ge(n2_ost[b], 16 * PAIRS_N)

            def l3_step(q, before):
                if q is not None:
                    ge(pool, l3["ts"], l3.at("ts", q.n - 2))
                    ge(pool, l3["xb"], l3.at("xb", q.n - 2))
                    indices(ixr[:, q.b], news_i, q.g * R, R, l3["ix"], 2 * q.g + 1)
                    indices(ixs[:, q.b], newd_i, q.g * R, R, l3["ix"], 2 * q.g + 2)
                    for r in range(R):
                        gather(gr[:, q.b, r, :], xC, ixr[:, q.b, r:r + 1], l3_got[q.b])
                        gather(at[:, q.b, r, :], xC, ixs[:, q.b, r:r + 1], l3_own[q.b])
                if before is not None:
                    pool.wait_ge(l3["var"], 3 * before.n)
                    ge(pool, l3["out"], l3.at("out", before.n - 1))
                    inverse_root(r2[:], vin2[:]).then_inc(l3["pw"], 1)
                    pool.wait_ge(l3["out"], l3.at("out", before.n))
                    after_wait(pool)
                    ge(pool, l3_put[before.b], 16 * R * before.i)
                    indices(put_at[:, before.b], skip_or_dst, before.g * R, R, l3_ix_put, before.n)
                    for r in range(R):
                        POOL.indirect_dma_start(
                            a["out"], bass.IndirectOffsetOnAxis(ap=put_at[:, before.b, r:r + 1], axis=0),
                            oA[:, before.b, r, :], None, bounds_check=N - 1,
                            oob_is_err=False).then_inc(l3_put[before.b], 16)
            edge_groups(POOL.Fori, l3_step)

        @block.tensor
        def _(pe):
            def transposes(out, src):
                for r in range(R):
                    mm = pe.transpose(out[:, r * P:(r + 1) * P], src(r), ident[:])
                return mm

            def rows_times(out, lhs, rhs):
                for r in range(R):
                    mm = pe.matmul(out[:, r * D:(r + 1) * D], lhs[:, r, :], rhs, start=True, stop=True)
                return mm

            def gram(bank, lhs, rhs):
                for r in range(R):
                    mm = pe.matmul(bank[:, 0:D + 1], lhs(r), rhs(r), start=False, stop=True, skip_group_check=True)
                return mm

            pe.wait_ge(pool_const, POOL_CONST)
            pe.wait_ge(const_loaded, CONST)
            pe.transpose(pm1[:, 0:D], W1[:], ident[:])
            pe.transpose(pm1[:, D:2 * D], W2[:], ident[:]).then_inc(setup_pe, 1)
            pe.matmul(pG[:, 0:D + 1], ident[:], gm[:, 0, :], start=True, stop=True)
            pe.wait_ge(setup_dve, ROWS_READY)
            for c in range(5):
                mm = pe.transpose(pm2[:, ET * c:ET * (c + 1)], rows_f[:, c, :], ident[0:ET, 0:ET])
            mm.then_inc(setup_pe, 1)

            def step(i, k, fr, mi, ba, ta, od, work=None):
                def mm3(c):
                    if c == 0:
                        pe.wait_ge(n2_made, ba.n)
                    ge(pe, gelu_made, 4 * ba.g + c - 1)
                    pe.matmul(pm3[c % 2][:], Wf1[:, c * P:(c + 1) * P], f(w["n2"][:]), start=True,
                              stop=True).then_inc(mm3_done, 1)

                if mi is not None:
                    if mi.kind == "N":
                        pe.wait_ge(h_made, mi.n)
                    else:
                        pe.wait_ge(he_made, mi.j + 1)
                    ge(pe, r_made, mi.n - 1)
                    if isinstance(mi.i, int) and mi.g == 0:
                        pe.wait_ge(setup_dve, SETUP_DVE)
                    pe.matmul(pm1[:], Wg1[:], f(w["h"][:]), start=True, stop=True).then_inc(mm1_done, 1)
                if ba is not None:
                    mm3(0)
                    mm3(1)
                if mi is not None:
                    pe.wait_ge(r_made, mi.n)
                    ge(pe, x1_made, mi.n - 1)
                    rows_times(pm2, w["r"], Wg2[:]).then_inc(mm2_done, 1)
                if ba is not None:
                    mm3(2)
                    mm3(3)
                if fr is not None and fr.kind == "E":
                    pe.wait_ge(xhs_made, fr.j + 1)
                    pe.wait_ge(h_made, NG)
                    ge(pe, hraw_made, fr.j)
                    transposes(pT1, lambda r: w["xhs"][:, r, :]).then_inc(ts_done, 1)
                    pe.wait_ge(attr_got[fr.b], 16 * R * (fr.i - NG // 2 + 1))
                    pe.wait_ge(n2_made, fr.n - 2)
                    transposes(pT2, lambda r: at[:, fr.b, r, :]).then_inc(ta_done, 1)
                if fr is not None:
                    pe.wait_ge(xh1_made, fr.n)
                    if fr.kind == "N":
                        ge(pe, h_made, fr.n - 1)
                    else:
                        pe.wait_ge(ms_made, fr.j + 1)
                    transposes(pT1, lambda r: w["xh1"][:, r, :]).then_inc(t1_done, 1)
                if ba is not None:
                    pe.wait_ge(gelu_made, 4 * ba.n)
                    ge(pe, u_made, ba.n - 1)
                    for r in range(R):
                        for c in range(4):
                            mm = pe.matmul(pm4[:, r * D:(r + 1) * D], gT[:, c, r * P:(r + 1) * P], Wf2[:, c, :],
                                           start=(c == 0), stop=(c == 3))
                    mm.then_inc(mm4_done, 1)
                if mi is not None:
                    pe.wait_ge(xh2_made, mi.n)
                    ge(pe, n2_made, mi.n - 1)
                    if fr is not None and fr.kind == "E":
                        pe.wait_ge(ma_made, fr.j + 1)
                    transposes(pT2, lambda r: w["xh2"][:, r, :]).then_inc(t2_done, 1)
            run_pipeline(nc.tensor.Fori, step)

            def l1_step(q, before):
                if q is not None:
                    pe.wait_ge(l1_got[q.b], 16 * R * (q.i + 1))
                    pe.wait_ge(l1["same"], l1.at("same", q.n))
                    ge(pe, l1["rows"], l1.at("rows", q.n - 1))
                    for r in range(R):
                        for c in range(R):
                            mm = pe.matmul(pm1[:, r * D:(r + 1) * D], gT[:, c, r * P:(r + 1) * P], gr[:, q.b, c, :],
                                           start=(c == 0), stop=(c == R - 1))
                    mm.then_inc(l1["sum"], 1)
            edge_groups(nc.tensor.Fori, l1_step)

            def nb_step(p, before):
                if before is not None:
                    pe.wait_ge(nb["m"], nb.at("m", before.n))
                    gram(pG, lambda r: oA[:, before.b, r, :], lambda r: gm[:, r, :]).then_inc(nb["gram"], 1)
            node_groups(nc.tensor.Fori, nb_step)

            pe.wait_ge(u_made, PIPE)
            pe.matmul(pm4[:, 0:D + 1], ident[:], zero_row[:, 0:D + 1], start=True, stop=True)

            def l2_step(q, before):
                if q is not None:
                    pe.wait_ge(l2_got[q.b], 16 * R * (q.i + 1))
                    ge(pe, l2["scan"], l2.at("scan", q.n - 1))
                    transposes(pT1, lambda r: gr[:, q.b, r, :]).then_inc(l2["t"], 1)
                    pe.wait_ge(l2["scan"], l2.at("scan", q.n))
                    ge(pe, l2["g"], l2.at("g", q.n - 1))
                    agg = w["f1"] if q.b else w["f0"]
                    transposes(pT2, lambda r: agg[:, r, :]).then_inc(l2["tb"], 1)
                if before is not None:
                    pe.wait_ge(l2["g"], l2.at("g", before.n))
                    ge(pe, l2["gt"], l2.at("gt", before.n - 1))
                    transposes(pm1, lambda r: ub[:, before.b, r, :]).then_inc(l2["tg"], 1)
                    pe.wait_ge(l2["gm"], l2.at("gm", before.n))
                    gram(pm4, lambda r: ub[:, before.b, r, :], lambda r: gm[:, r, :]).then_inc(l2["gram"], 1)
                    pe.wait_ge(l2["gt"], l2.at("gt", before.n))
                    ge(pe, l2["h"], l2.at("h", before.n - 1))
                    pe.matmul(pm2[:], W1T[:], f(w["n2"][:]), start=True, stop=True).then_inc(l2["mm"], 1)
            edge_groups(nc.tensor.Fori, l2_step)

            pe.wait_ge(bns["dve"], BN_COV)
            pe.matmul(pm1[:, 0:D], cov[:, 0:D], W1T[:], start=True, stop=True)
            pe.matmul(pm1[:, D:D + 1], W1T[:], cov[:, D:D + 1], start=True, stop=True).then_inc(bns["pe"], 1)
            pe.wait_ge(bns["dve"], BN_QUAD)
            pe.matmul(pm3[0][:, 0:1], covE[:, 0:D], ones[:, 0:1], start=True, stop=True).then_inc(bns["pe"], 1)

            def q2_step(q, before):
                if q is not None:
                    pe.wait_ge(q2["r"], q2.at("r", q.n))
                    ge(pe, q2["t"], q2.at("t", q.n - 1))
                    pe.wait_ge(l2["h"], l2.at("h", EG))
                    rows_times(pm2, w["r"], W2T[:]).then_inc(q2["mm"], 1)
            edge_groups(nc.tensor.Fori, q2_step)

            def n2_step(p, before):
                if p is not None:
                    pe.wait_ge(n2_loaded[p.b], 16 * (p.i + 1))
                    ge(pe, n2["c"], n2.at("c", p.n - 1))
                    transposes(pT1, lambda r: xin[:, p.b, r, :]).then_inc(n2["ta"], 1)
                    pe.wait_ge(n2["c"], n2.at("c", p.n))
                    ge(pe, n2["r"], n2.at("r", p.n - 1))
                    pe.matmul(pm1[:], W1T[:], f(w["h"][:]), start=True, stop=True).then_inc(n2["mm1"], 1)
                if before is not None:
                    pe.wait_ge(n2["xc"], n2.at("xc", before.n))
                    ge(pe, n2["ct"], n2.at("ct", before.n - 1))
                    transposes(pT2, lambda r: oA[:, before.b, r, :]).then_inc(n2["tc"], 1)
                if p is not None:
                    pe.wait_ge(n2["r"], n2.at("r", p.n))
                    ge(pe, n2["t"], n2.at("t", p.n - 1))
                    rows_times(pm2, w["r"], W2T[:]).then_inc(n2["mm2"], 1)
                if before is not None:
                    pe.wait_ge(n2["ct"], n2.at("ct", before.n))
                    ge(pe, n2["z"], n2.at("z", before.n - 1))
                    rows_times(pm4, w["n2"], Ws[:]).then_inc(n2["mm3"], 1)
            node_groups(nc.tensor.Fori, n2_step)

            def l3_step(q, before):
                if q is not None:
                    pe.wait_ge(l3_got[q.b], 16 * R * (q.i + 1))
                    ge(pe, l3["xs"], l3.at("xs", q.n - 1))
                    transposes(pT1, lambda r: gr[:, q.b, r, :]).then_inc(l3["ts"], 1)
                    pe.wait_ge(l3_own[q.b], 16 * R * (q.i + 1))
                    ge(pe, l3["xd"], l3.at("xd", q.n - 1))
                    transposes(pT2, lambda r: at[:, q.b, r, :]).then_inc(l3["td"], 1)
                    pe.wait_ge(l3["xd"], l3.at("xd", q.n))
                    ge(pe, l3["q"], l3.at("q", q.n - 1))
                    pe.matmul(pm1[:], Wq[:], f(w["n2"][:]), start=True, stop=True).then_inc(l3["mq"], 1)
                    pe.wait_ge(l3["xs"], l3.at("xs", q.n))
                    ge(pe, l3["qk"], l3.at("qk", q.n - 1))
                    pe.matmul(pm2[:], Wk[:], f(w["h"][:]), start=True, stop=True).then_inc(l3["mk"], 1)
                    ge(pe, l3["num"], l3.at("num", q.n - 1))
                    pe.matmul(pm3[0][:], Wv[:], f(w["h"][:]), start=True, stop=True).then_inc(l3["mv"], 1)
                    pe.wait_ge(l3["qk"], l3.at("qk", q.n))
                    ge(pe, l3["l"], l3.at("l", q.n - 1))
                    pe.matmul(pm3[1][:], ones[:], f(w["msg"][:]), start=True, stop=True).then_inc(l3["ml"], 1)
                    pe.wait_ge(l3["o"], l3.at("o", q.n))
                    ge(pe, l3["z"], l3.at("z", q.n - 1))
                    for r in range(R):
                        pe.matmul(pm4[:, r * D:(r + 1) * D], w["n2"][:, r, :], Ws[:], start=True, stop=False)
                        mm = pe.matmul(pm4[:, r * D:(r + 1) * D], w["ma"][:, r, :], ident[:], start=False, stop=True)
                    mm.then_inc(l3["mm"], 1)
            edge_groups(nc.tensor.Fori, l3_step)

        @block.scalar
        def _(act):
            A = nc.scalar
            act.wait_ge(const_loaded, CONST)
            act.wait_ge(setup_dve, SETUP_DVE)
            act.wait_ge(pool_const, POOL_CONST)

            def scale_rows(out, src, scale, bias):
                for r in range(R):
                    last = A.activation(out(r), src(r), ACT.Identity, bias=bias(r), scale=scale(r))
                return last

            def step(i, k, fr, mi, ba, ta, od, work=None):
                def gelu(c):
                    if c == 0:
                        ge(act, mm4_done, ba.n - 1)
                    act.wait_ge(mm3_done, 4 * ba.g + c + 1)
                    A.activation(gT[:, c, :], pm3[c % 2][:], ACT.Gelu, bias=bf1c[:, c:c + 1]).then_inc(gelu_made, 1)

                if mi is not None:
                    act.wait_ge(mm1_done, mi.n)
                    ge(act, mm2_done, mi.n - 1)
                    A.activation(f(w["r"][:]), pm1[:], ACT.Relu, bias=col["bg1"]).then_inc(r_made, 1)
                if ba is not None:
                    gelu(0)
                    gelu(1)
                if ta is not None:
                    act.wait_ge(nma_made, ta.n)
                    if ta.kind == "N":
                        ge(act, xA_stored[ta.b], 16 * ta.i)
                        out = lambda r: oA[:, ta.b, r, :]
                    else:
                        out = lambda r: tile(X, ta.j, r)
                    scale_rows(out, lambda r: ub[:, ta.b, r, :], lambda r: r3[:, ta.b, r:r + 1],
                               lambda r: nma[:, r:r + 1]).then_inc(xA_made, 1)
                if ba is not None:
                    gelu(2)
                    gelu(3)
                if fr is not None and fr.kind == "E":
                    act.wait_ge(ts_done, fr.j + 1)
                    ge(act, ma_made, fr.j)
                    A.activation(f(w["ms"][:]), pT1[:], ACT.Identity, bias=col["b1"], scale=col["g1"]).then_inc(ms_made, 1)
                if fr is not None:
                    act.wait_ge(t1_done, fr.n)
                    if fr.kind == "N":
                        ge(act, mm1_done, fr.n - 1)
                        A.activation(f(w["h"][:]), pT1[:], ACT.Identity, bias=b1s, scale=g1s).then_inc(h_made, 1)
                    else:
                        ge(act, he_made, fr.j)
                        A.activation(f(w["hraw"][:]), pT1[:], ACT.Identity, bias=b1s, scale=g1s).then_inc(hraw_made, 1)
                        act.wait_ge(ma_made, fr.j + 1)
                        ge(act, agg_made, fr.j)
                        A.activation(f(w["msg"][:]), f(w["ma"][:]), ACT.Relu).then_inc(msg_made, 1)
                if ta is not None:
                    act.wait_ge(nmb_made, 2 * ta.n)
                    if ta.kind == "N":
                        ge(act, y_stored[ta.b], 16 * ta.i)
                    else:
                        act.wait_ge(y_stored[ta.b], 16 * PAIRS_N)
                        ge(act, y_put[ta.b], 16 * R * (ta.i - NG // 2))
                    scale_rows(lambda r: oB[:, ta.b, r, :], lambda r: ub[:, ta.b, r, :],
                               lambda r: rb[:, r:r + 1], lambda r: nmb[:, r:r + 1]).then_inc(y_made, 1)
                if mi is not None:
                    act.wait_ge(t2_done, mi.n)
                    ge(act, mm3_done, 4 * (mi.n - 1))
                    A.activation(f(w["n2"][:]), pT2[:], ACT.Identity, bias=col["b2"], scale=col["g2"]).then_inc(n2_made, 1)

            run_pipeline(A.Fori, step)

            def l1_step(q, before):
                if q is not None:
                    act.wait_ge(l1["sum"], l1.at("sum", q.n))
                    ge(act, l1_added[q.b], 16 * R * q.i)
                    for b in range(2):
                        act.wait_ge(xA_stored[b], 16 * PAIRS_N)
                    A.copy(f(oA[:, q.b]), pm1[:]).then_inc(l1["rows"], 1)
            edge_groups(A.Fori, l1_step)

            def nb_step(p, before):
                if before is not None:
                    act.wait_ge(nb["x"], nb.at("x", before.n))
                    ge(act, nb["gram"], nb.at("gram", before.n - 1))
                    A.copy(gm[:, :, D:D + 1].rearrange("p r o -> p (r o)"), open_rows[:, span(before.g, 1), :].rearrange("p o r -> p (o r)"))
                    for r in range(R):
                        last = A.activation(gm[:, r, 0:D], oA[:, before.b, r, :], ACT.Identity,
                                            scale=open_rows[:, span(before.g, 1), r:r + 1].rearrange("p o r -> p (o r)"))
                    last.then_inc(nb["m"], 1)
            node_groups(A.Fori, nb_step)

            def l2_step(q, before):
                if q is not None:
                    act.wait_ge(l2_own[q.b], 16 * R * (q.i + 1))
                    A.copy(X[:, span(q.g * R, R), :], at[:, q.b]).then_inc(l2["x"], 1)
                if before is not None:
                    act.wait_ge(nb["gram"], NG)
                    act.wait_ge(l2["g"], l2.at("g", before.n))
                    ge(act, l2["gram"], l2.at("gram", before.n - 1))
                    A.copy(gm[:, :, D:D + 1].rearrange("p r o -> p (r o)"), is_last[:, span(before.g * R, R)])
                    for r in range(R):
                        last = A.activation(gm[:, r, 0:D], ub[:, before.b, r, :], ACT.Identity,
                                            scale=is_last[:, span(before.g * R + r, 1)])
                    last.then_inc(l2["gm"], 1)
                    act.wait_ge(l2["tg"], l2.at("tg", before.n))
                    ge(act, l2["mm"], l2.at("mm", before.n - 1))
                    A.copy(f(w["n2"][:]), pm1[:]).then_inc(l2["gt"], 1)
                    act.wait_ge(l2["mm"], l2.at("mm", before.n))
                    A.copy(HT[:, span(before.g * G, G)], pm2[:]).then_inc(l2["h"], 1)
            edge_groups(A.Fori, l2_step)

            act.wait_ge(bns["ready"], BN_DONE)

            def q2_step(q, before):
                if q is not None:
                    ge(act, q2["mm"], q2.at("mm", q.n - 1))
                    act.wait_ge(l2["h"], l2.at("h", EG))
                    A.activation(f(w["r"][:]), HT[:, span(q.g * G, G)], ACT.Relu, bias=bn_b, scale=bn_a).then_inc(q2["r"], 1)
                    act.wait_ge(q2["t"], q2.at("t", q.n))
                    ge(act, q2["y"], q2.at("y", q.n - 1))
                    A.activation(w["ms"][:], w["x1"][:], ACT.Relu).then_inc(q2["rt"], 1)
            edge_groups(A.Fori, q2_step)

            def n2_step(p, before):
                if p is not None:
                    act.wait_ge(n2["ta"], n2.at("ta", p.n))
                    ge(act, n2["mm1"], n2.at("mm1", p.n - 1))
                    A.activation(f(w["h"][:]), pT1[:], ACT.Identity, scale=one_e2).then_inc(n2["c"], 1)
                    act.wait_ge(n2["mm1"], n2.at("mm1", p.n))
                    ge(act, n2["mm2"], n2.at("mm2", p.n - 1))
                    A.activation(f(w["r"][:]), pm1[:], ACT.Relu, bias=bn_b, scale=bn_a).then_inc(n2["r"], 1)
                if before is not None:
                    act.wait_ge(n2["tc"], n2.at("tc", before.n))
                    ge(act, n2["mm3"], n2.at("mm3", before.n - 1))
                    A.copy(f(w["n2"][:]), pT2[:]).then_inc(n2["ct"], 1)
                if p is not None:
                    act.wait_ge(n2["t"], n2.at("t", p.n))
                    ge(act, n2["y"], n2.at("y", p.n - 1))
                    A.activation(w["ms"][:], w["x1"][:], ACT.Relu).then_inc(n2["rt"], 1)
                if before is not None:
                    act.wait_ge(n2["nm"], n2.at("nm", before.n))
                    ge(act, n2_ost[before.b], 16 * before.i)
                    scale_rows(lambda r: s2b[:, before.b, r, :], lambda r: ub[:, before.b, r, :],
                               lambda r: r3[:, before.b, r:r + 1], lambda r: nma[:, r:r + 1]).then_inc(n2["o"], 1)
            node_groups(A.Fori, n2_step)

            def l3_step(q, before):
                if q is not None:
                    act.wait_ge(l3["ts"], l3.at("ts", q.n))
                    ge(act, l3["mv"], l3.at("mv", q.n - 1))
                    A.copy(f(w["h"][:]), pT1[:]).then_inc(l3["xs"], 1)
                    act.wait_ge(l3["td"], l3.at("td", q.n))
                    ge(act, l3["mm"], l3.at("mm", q.n - 1))
                    A.copy(f(w["n2"][:]), pT2[:]).then_inc(l3["xd"], 1)
                    act.wait_ge(l3["mq"], l3.at("mq", q.n))
                    ge(act, l3["qk"], l3.at("qk", q.n - 1))
                    A.activation(f(w["r"][:]), pm1[:], ACT.Identity, bias=col["bq"]).then_inc(l3["q"], 1)
                    ge(act, l3["e1"], l3.at("e1", q.n - 1))
                    A.activation(f(w["hraw"][:]), keep[:, span(q.g * G, G)], ACT.Identity, bias=mbig[:], scale=BIG).then_inc(l3["pen"], 1)
                    act.wait_ge(l3["ml"], l3.at("ml", q.n))
                    ge(act, l3["lm"], l3.at("lm", q.n - 1))
                    A.activation(f(w["ms"][:]), pm3[1][:], ACT.Identity, scale=SM_SCALE).then_inc(l3["l"], 1)
                    act.wait_ge(l3["e2"], l3.at("e2", q.n))
                    ge(act, l3["den"], l3.at("den", q.n - 1))
                    A.activation(f(w["xb"][:]), f(w["x1"][:]), ACT.Exp).then_inc(l3["c"], 1)
                    act.wait_ge(l3["lm"], l3.at("lm", q.n))
                    A.activation(f(w["xc"][:]), f(w["xh2"][:]), ACT.Exp).then_inc(l3["p"], 1)
            edge_groups(A.Fori, l3_step)

        @block.vector
        def _(dve):
            V = nc.vector

            def stats(src, k, s, n):
                for r in range(R):
                    last = V.bn_stats(stt[:, k, r, :], src(r))
                last.then_inc(s, 1)
                dve.wait_ge(s, 3 * n - 2)
                after_wait(dve)
                for r in range(R):
                    last = V.bn_aggr(mv[:, k, r, :], stt[:, k, r, :])
                last.then_inc(s, 1)
                dve.wait_ge(s, 3 * n - 1)

            def normalise(out, src, k, scale):
                for r in range(R):
                    last = V.tensor_scalar(out(r), src(r), mv[:, k, r, 0:1], scale[:, r:r + 1], ALU.subtract, ALU.mult)
                return last

            def variance(out, k):
                return V.tensor_scalar(out, mv[:, k, :, 1], LN_EPS, None, ALU.add)

            dve.wait_ge(const_loaded, CONST)
            V.tensor_scalar(one_eg, eps3[:, 0:1], 1.0, None, ALU.add).then_inc(setup_dve, 1)
            V.tensor_scalar(two_e1, eps3[:, 1:2], 2.0, None, ALU.add).then_inc(setup_dve, 1)
            V.tensor_scalar(one_e2, eps3[:, 2:3], 1.0, None, ALU.add).then_inc(setup_dve, 1)
            V.memset(zero_row[:], 0.0).then_inc(setup_dve, 1)
            dve.wait_ge(pool_const, POOL_CONST)
            V.tensor_copy(spare[:], spare_i[:]).then_inc(setup_dve, 1)
            V.memset(mbig[:], -BIG).then_inc(setup_dve, 1)
            dve.wait_ge(setup_dve, 6)
            V.tensor_tensor(g1s, col["g1"], one_eg, ALU.mult).then_inc(setup_dve, 1)
            V.tensor_tensor(b1s, col["b1"], one_eg, ALU.mult).then_inc(setup_dve, 1)
            V.tensor_tensor(two_e1sq, two_e1, two_e1, ALU.mult).then_inc(setup_dve, 1)
            dve.wait_ge(rows_loaded, 16 * 4)
            V.tensor_copy(rows_f[:, 5, :], rows_i[:, 0, :]).then_inc(setup_dve, 1)
            V.tensor_copy(rows_f[:, 6, :], rows_i[:, 1, :]).then_inc(setup_dve, 1)
            V.tensor_copy(rows_f[:, 2, :], rows_i[:, 2, :]).then_inc(setup_dve, 1)
            V.tensor_copy(rows_f[:, 7, :], rows_i[:, 3, :]).then_inc(setup_dve, 1)
            dve.wait_ge(setup_dve, 13)
            V.tensor_tensor(rows_f[:, 4, :], rows_f[:, 5, :], rows_f[:, 6, :], ALU.is_equal).then_inc(setup_dve, 1)
            dve.wait_ge(setup_dve, 14)
            V.scalar_tensor_tensor(out=rows_f[:, 0, :], in0=rows_f[:, 4, :], scalar=float(FAR), in1=rows_f[:, 5, :],
                                   op0=ALU.mult, op1=ALU.add).then_inc(setup_dve, 1)
            V.tensor_scalar(rows_f[:, 1, :], rows_f[:, 5, :], float(N - 1), None, ALU.min).then_inc(setup_dve, 1)
            V.tensor_scalar(rows_f[:, 3, :], rows_f[:, 7, :], float(E - 1), None, ALU.min).then_inc(setup_dve, 1)
            dve.wait_ge(setup_pe, 1)
            V.tensor_copy(W1T[:], pm1[:, 0:D]).then_inc(setup_dve, 1)
            V.tensor_copy(W2T[:], pm1[:, D:2 * D]).then_inc(setup_dve, 1)
            dve.wait_ge(setup_pe, 2)
            for t, c in ((skip_or_dst, 0), (dst_i, 1), (perm_i, 3)):
                V.tensor_copy(t[:], pm2[:, ET * c:ET * (c + 1)]).then_inc(setup_dve, 1)
            V.tensor_scalar(is_last[:], pm2[:, 4 * ET:5 * ET], -1.0, 1.0, ALU.mult, ALU.add).then_inc(setup_dve, 1)
            V.tensor_copy(src_f[:], pm2[:, 2 * ET:3 * ET]).then_inc(setup_dve, 1)
            V.tensor_scalar(src_i[:], pm2[:, 2 * ET:3 * ET], float(N - 1), None, ALU.min).then_inc(setup_dve, 1)
            dve.wait_ge(setup_dve, SETUP_DVE)
            V.memset(carry[:], 0.0).then_inc(idx_ready, 1)
            for c in range(KC):
                dve.wait_ge(dstb_loaded[c % 2], 16 * (c // 2 + 1))
                V.tensor_tensor(keep[:, c * KW:(c + 1) * KW], dstb[c % 2][:, 1:KW + 1], dstb[c % 2][:, 0:KW],
                                ALU.is_equal).then_inc(keep_made, 1)
            dve.wait_ge(keep_made, KC)
            dve.wait_ge(pool_const, POOL_CONST)

            def step(i, k, fr, mi, ba, ta, od, work=None):
                if ta is not None:
                    dve.wait_ge(pow3, ta.n)
                    ge(dve, xA_made, ta.n - 1)
                    V.scalar_tensor_tensor(out=nma[:], in0=mv[:, 2, :, 0], scalar=-1.0, in1=r3[:, ta.b],
                                           op0=ALU.mult, op1=ALU.mult).then_inc(nma_made, 1)
                    ge(dve, y_made, ta.n - 1)
                    V.tensor_scalar(rb[:], r3[:, ta.b], two_e1, None, ALU.mult).then_inc(nmb_made, 1)
                    dve.wait_ge(nma_made, ta.n)
                    V.tensor_scalar(nmb[:], nma[:], two_e1, None, ALU.mult).then_inc(nmb_made, 1)
                if fr is not None:
                    if fr.kind == "N":
                        dve.wait_ge(x_loaded[fr.b], 16 * (fr.i + 1))
                        x, xall = (lambda r: xin[:, fr.b, r, :]), xin[:, fr.b]
                    else:
                        dve.wait_ge(pre_kept[0], 16 * EG)
                        dve.wait_ge(pre_kept[1], 16 * EG)
                        x, xall = (lambda r: tile(X, fr.j, r)), X[:, span(fr.j * R, R), :]
                        stats(lambda r: tile(H, fr.j, r), 3, var["s"], fr.j + 1)
                        variance(vinc[:, 8:12], 3).then_inc(var["s"], 1)
                    stats(x, 0, var["1"], fr.n)
                    variance(vinc[:, 0:4], 0).then_inc(var["1"], 1)
                if mi is not None:
                    dve.wait_ge(mm2_done, mi.n)
                    dve.wait_ge(xb_made, mi.n)
                    ge(dve, s_made, mi.n - 1)
                    V.tensor_tensor(f(w["x1"][:]), pm2[:], f(w["xb"][:]), ALU.add).then_inc(x1_made, 1)
                    dve.wait_ge(x1_made, mi.n)
                    stats(lambda r: w["x1"][:, r, :], 1, var["2"], mi.n)
                    variance(vin2[:], 1).then_inc(var["2"], 1)
                if fr is not None:
                    dve.wait_ge(powc, fr.n)
                    if fr.kind == "E":
                        ge(dve, ts_done, fr.j)
                        normalise(lambda r: w["xhs"][:, r, :], lambda r: tile(H, fr.j, r), 3, ro[:, 8:12]).then_inc(xhs_made, 1)
                    ge(dve, t1_done, fr.n - 1)
                    normalise(lambda r: w["xh1"][:, r, :], x, 0, ro[:, 0:4]).then_inc(xh1_made, 1)
                    V.tensor_tensor(w["xb"][:], xall, bcast(bg2r), ALU.add).then_inc(xb_made, 1)
                if mi is not None:
                    dve.wait_ge(pow2, mi.n)
                    ge(dve, t2_done, mi.n - 1)
                    normalise(lambda r: w["xh2"][:, r, :], lambda r: w["x1"][:, r, :], 1, r2).then_inc(xh2_made, 1)
                if fr is not None and fr.kind == "E":
                    dve.wait_ge(ms_made, fr.j + 1)
                    dve.wait_ge(ta_done, fr.j + 1)
                    ge(dve, msg_made, fr.j)
                    V.tensor_tensor(f(w["ma"][:]), pT2[:], f(w["ms"][:]), ALU.add).then_inc(ma_made, 1)
                if ba is not None:
                    dve.wait_ge(mm4_done, ba.n)
                    dve.wait_ge(s_made, ba.n)
                    V.tensor_tensor(f(ub[:, ba.b]), pm4[:], f(s2b[:, ba.b]), ALU.add).then_inc(u_made, 1)
                    dve.wait_ge(u_made, ba.n)
                    stats(lambda r: ub[:, ba.b, r, :], 2, var["3"], ba.n)
                    variance(vin3[:], 2).then_inc(var["3"], 1)
                if fr is not None and fr.kind == "E":
                    dve.wait_ge(msg_made, fr.j + 1)
                    agg, before = (w["f1"], w["f0"]) if fr.b else (w["f0"], w["f1"])
                    if isinstance(fr.i, int) and fr.j == 0:
                        first = 0.0
                    else:
                        first = before[:, R - 1, D - 1:D]
                        dve.wait_ge(agg_made, fr.j)
                    V.tensor_tensor_scan(f(agg[:]), keep[:, span(fr.j * G, G)], f(w["msg"][:]), first,
                                         ALU.mult, ALU.add).then_inc(agg_made, 1)
                    dve.wait_ge(agg_made, fr.j + 1)
                    dve.wait_ge(hraw_made, fr.j + 1)
                    dve.wait_ge(mm1_done, fr.n - 1)
                    V.tensor_tensor(w["h"][:], w["hraw"][:], agg[:], ALU.add).then_inc(he_made, 1)

            run_pipeline(V.Fori, step)

            def l1_step(q, before):
                if q is not None:
                    dve.wait_ge(l1_keys[q.b], 16 * (q.i + 1))
                    ge(dve, l1["sum"], l1.at("sum", q.n - 1))
                    for r in range(R):
                        last = V.tensor_scalar(gT[:, r, :], keys[:, q.b], src_f[:, span(q.g * R + r, 1)], None, ALU.is_equal)
                    last.then_inc(l1["same"], 1)
                    dve.wait_ge(l1["same"], l1.at("same", q.n))
                    for r in range(R):
                        last = V.tensor_tensor_reduce(out=l1_junk[r], in0=gT[:, r, :], in1=later_mask[:, r, :], scale=1.0,
                                                      scalar=0.0, op0=ALU.mult, op1=ALU.add, accum_out=sm[:, 0, r:r + 1])
                    last.then_inc(l1["count"], 1)
                    own = src_f[:, span(q.g * R, R)]
                    V.tensor_scalar(sm[:, 1, :], own, float(N), None, ALU.is_ge).then_inc(l1["far"], 1)
                    dve.wait_ge(l1["far"], l1.at("far", q.n))
                    V.scalar_tensor_tensor(out=sm[:, 2, :], in0=sm[:, 0, :], scalar=0.0, in1=sm[:, 1, :],
                                           op0=ALU.is_gt, op1=ALU.max).then_inc(l1["dup"], 1)
                    V.tensor_tensor(sm[:, 3, :], spare[:], own, ALU.subtract).then_inc(l1["away"], 1)
                    dve.wait_ge(l1["away"], l1.at("away", q.n))
                    V.tensor_tensor(sm[:, 4, :], sm[:, 3, :], sm[:, 2, :], ALU.mult).then_inc(l1["mul"], 1)
                    dve.wait_ge(l1["mul"], l1.at("mul", q.n))
                    ge(dve, l1_added[q.b], 16 * R * q.i)
                    V.tensor_tensor(sums_at[:, q.b, 0:R], sm[:, 4, :], own, ALU.add).then_inc(l1["idx"], 1)
            dve.wait_ge(later_made, 2)
            for b in range(2):
                dve.wait_ge(y_put[b], 16 * R * ((EG + 1 - b) // 2))
            edge_groups(V.Fori, l1_step)

            dve.wait_ge(open_loaded, 16 * NG)
            V.tensor_scalar(open_rows[:], open_i[:], float(N), None, ALU.is_lt).then_inc(bns["open"], 1)
            dve.wait_ge(bns["open"], 1)
            V.tensor_scalar(open_rows[:, NG - 1, :], open_rows[:, NG - 1, :], fresh[:], None, ALU.mult).then_inc(bns["open"], 1)
            dve.wait_ge(l1["rows"], l1.at("rows", EG))
            for b in range(2):
                dve.wait_ge(l1_added[b], 16 * R * ((EG + 1 - b) // 2))

            def nb_step(p, before):
                if p is not None:
                    dve.wait_ge(nb_loaded[p.b], 16 * (p.i + 1))
                    stats(lambda r: xin[:, p.b, r, :], 1, nb["var"], p.n)
                    variance(vin2[:], 1).then_inc(nb["var"], 1)
                    dve.wait_ge(nb["pw"], nb.at("pw", p.n))
                    ge(dve, nb_stored[p.b], 16 * p.i)
                    ge(dve, nb["gram"], nb.at("gram", p.n - 2))
                    normalise(lambda r: oA[:, p.b, r, :], lambda r: xin[:, p.b, r, :], 1, r2).then_inc(nb["x"], 1)
            node_groups(V.Fori, nb_step)

            def scanned(q, s, n):
                agg, before = (w["f1"], w["f0"]) if q.b else (w["f0"], w["f1"])
                if isinstance(q.i, int) and q.g == 0:
                    first = 0.0
                else:
                    first = before[:, R - 1, D - 1:D]
                    dve.wait_ge(s["scan"], s.at("scan", n - 1))
                V.tensor_tensor_scan(f(agg[:]), keep[:, span(q.g * G, G)], pT1[:], first,
                                     ALU.mult, ALU.add).then_inc(s["scan"], 1)

            def l2_step(q, before):
                if q is not None:
                    dve.wait_ge(l2["t"], l2.at("t", q.n))
                    ge(dve, l2["tb"], l2.at("tb", q.n - 2))
                    scanned(q, l2, q.n)
                    dve.wait_ge(l2["tb"], l2.at("tb", q.n))
                    dve.wait_ge(l2_own[q.b], 16 * R * (q.i + 1))
                    ge(dve, l2["gram"], l2.at("gram", q.n - 2))
                    ge(dve, l2["gm"], l2.at("gm", q.n - 2))
                    V.scalar_tensor_tensor(out=ub[:, q.b], in0=at[:, q.b], scalar=one_e2,
                                           in1=pT2[:].rearrange("p (r d) -> p r d", r=R), op0=ALU.mult,
                                           op1=ALU.add).then_inc(l2["g"], 1)
            edge_groups(V.Fori, l2_step)

            dve.wait_ge(l2["gram"], l2.at("gram", EG))
            dve.wait_ge(nb["gram"], NG)
            B, dn = bns["dve"], [0]

            def chain(ins):
                ins.then_inc(B, 1)
                dn[0] += 1
                dve.wait_ge(B, dn[0])
            chain(V.tensor_copy(covE[:], pm4[:, 0:D + 1]))
            chain(V.tensor_scalar(cov[:], pG[:, 0:D + 1], one_e2, None, ALU.mult))
            chain(V.scalar_tensor_tensor(out=cov[:, 0:D], in0=cov[:, 0:D], scalar=one_e2, in1=covE[:, 0:D],
                                         op0=ALU.mult, op1=ALU.add))
            chain(V.tensor_tensor(cov[:, D:D + 1], cov[:, D:D + 1], covE[:, D:D + 1], ALU.add))
            chain(V.tensor_scalar(cov[:], cov[:], 1.0 / N, None, ALU.mult))
            assert dn[0] == BN_COV
            dve.wait_ge(bns["pe"], 1)
            chain(V.tensor_tensor(covE[:, 0:D], pm1[:, 0:D], W1T[:], ALU.mult))
            chain(V.tensor_copy(bn[:, 0:1], pm1[:, D:D + 1]))
            assert dn[0] == BN_QUAD
            dve.wait_ge(bns["pe"], 2)
            chain(V.tensor_tensor(bn[:, 1:2], bn[:, 0:1], bn[:, 0:1], ALU.mult))
            chain(V.tensor_copy(bn[:, 2:3], pm3[0][:, 0:1]))
            chain(V.tensor_tensor(bn[:, 3:4], bn[:, 2:3], bn[:, 1:2], ALU.subtract))
            chain(V.tensor_scalar(bn[:, 4:5], bn[:, 3:4], 0.0, BN_EPS, ALU.max, ALU.add))
            assert dn[0] == BN_VAR
            dve.wait_ge(bns["pw"], 1)
            chain(V.tensor_tensor(bn_a, bn[:, 5:6], col["gamma"], ALU.mult))
            chain(V.tensor_tensor(bn[:, 6:7], bn[:, 0:1], col["L2b1"], ALU.add))
            chain(V.tensor_tensor(bn[:, 7:8], col["L2b1"], bn[:, 6:7], ALU.subtract))
            chain(V.tensor_tensor(bn[:, 8:9], bn[:, 7:8], bn_a, ALU.mult))
            V.tensor_tensor(bn_b, bn[:, 8:9], col["beta"], ALU.add).then_inc(bns["ready"], BN_DONE)

            dve.wait_ge(l2["x"], EG)

            def q2_step(q, before):
                if q is not None:
                    dve.wait_ge(q2["mm"], q2.at("mm", q.n))
                    ge(dve, q2["rt"], q2.at("rt", q.n - 1))
                    V.tensor_tensor(w["x1"][:], pm2[:].rearrange("p (r d) -> p r d", r=R), bcast(b2r), ALU.add).then_inc(q2["t"], 1)
                if before is not None:
                    dve.wait_ge(q2["pw"], q2.at("pw", before.n))
                    normalise(lambda r: tile(X, before.g, r), lambda r: ub[:, before.b, r, :], 1, r2).then_inc(q2["x"], 1)
                if q is not None:
                    dve.wait_ge(q2["rt"], q2.at("rt", q.n))
                    V.scalar_tensor_tensor(out=ub[:, q.b], in0=X[:, span(q.g * R, R), :], scalar=2.0, in1=w["ms"][:],
                                           op0=ALU.mult, op1=ALU.add).then_inc(q2["y"], 1)
                    dve.wait_ge(q2["y"], q2.at("y", q.n))
                    stats(lambda r: ub[:, q.b, r, :], 1, q2["var"], q.n)
                    variance(vin2[:], 1).then_inc(q2["var"], 1)
            edge_groups(V.Fori, q2_step)

            def n2_step(p, before):
                if p is not None:
                    dve.wait_ge(n2["mm2"], n2.at("mm2", p.n))
                    ge(dve, n2["rt"], n2.at("rt", p.n - 1))
                    V.tensor_tensor(w["x1"][:], pm2[:].rearrange("p (r d) -> p r d", r=R), bcast(b2r), ALU.add).then_inc(n2["t"], 1)
                if before is not None:
                    dve.wait_ge(n2["mm3"], n2.at("mm3", before.n))
                    dve.wait_ge(n2["xcb"], n2.at("xcb", before.n))
                    ge(dve, n2["o"], n2.at("o", before.n - 2))
                    V.tensor_tensor(f(ub[:, before.b]), pm4[:], f(w["xb"][:]), ALU.add).then_inc(n2["z"], 1)
                    dve.wait_ge(n2["z"], n2.at("z", before.n))
                    stats(lambda r: ub[:, before.b, r, :], 2, n2["var2"], before.n)
                    variance(vin3[:], 2).then_inc(n2["var2"], 1)
                if p is not None:
                    dve.wait_ge(n2["rt"], n2.at("rt", p.n))
                    dve.wait_ge(n2_loaded[p.b], 16 * (p.i + 1))
                    V.scalar_tensor_tensor(out=w["xh1"][:], in0=xin[:, p.b], scalar=2.0, in1=w["ms"][:],
                                           op0=ALU.mult, op1=ALU.add).then_inc(n2["y"], 1)
                    dve.wait_ge(n2["y"], n2.at("y", p.n))
                    stats(lambda r: w["xh1"][:, r, :], 1, n2["var"], p.n)
                    variance(vin2[:], 1).then_inc(n2["var"], 1)
                if before is not None:
                    dve.wait_ge(n2["pw2"], n2.at("pw2", before.n))
                    ge(dve, n2["o"], n2.at("o", before.n - 1))
                    V.scalar_tensor_tensor(out=nma[:], in0=mv[:, 2, :, 0], scalar=-1.0, in1=r3[:, before.b],
                                           op0=ALU.mult, op1=ALU.mult).then_inc(n2["nm"], 1)
                if p is not None:
                    dve.wait_ge(n2["pw"], n2.at("pw", p.n))
                    ge(dve, n2_cst[p.b], 16 * p.i)
                    ge(dve, n2["tc"], n2.at("tc", p.n - 2))
                    ge(dve, n2["xcb"], n2.at("xcb", p.n - 2))
                    normalise(lambda r: oA[:, p.b, r, :], lambda r: w["xh1"][:, r, :], 1, r2).then_inc(n2["xc"], 1)
            node_groups(V.Fori, n2_step)

            for b in range(2):
                dve.wait_ge(n2_cst[b], 16 * PAIRS_N)

            def l3_step(q, before):
                if q is not None:
                    n = q.n
                    dve.wait_ge(l3["mk"], l3.at("mk", n))
                    dve.wait_ge(l3["q"], l3.at("q", n))
                    ge(dve, l3["ml"], l3.at("ml", n - 1))
                    V.scalar_tensor_tensor(out=f(w["msg"][:]), in0=pm2[:], scalar=col["bk"], in1=f(w["r"][:]),
                                           op0=ALU.add, op1=ALU.mult).then_inc(l3["qk"], 1)
                if before is not None:
                    dve.wait_ge(l3["pw"], l3.at("pw", before.n))
                    ge(dve, l3_put[before.b], 16 * R * before.i)
                    normalise(lambda r: oA[:, before.b, r, :], lambda r: ub[:, before.b, r, :], 1, r2).then_inc(l3["out"], 1)
                if q is not None:
                    M, Mb = (w["f1"], w["f0"]) if q.b else (w["f0"], w["f1"])
                    dve.wait_ge(l3["l"], l3.at("l", n))
                    dve.wait_ge(l3["pen"], l3.at("pen", n))
                    first = isinstance(q.i, int) and q.g == 0
                    if not first:
                        dve.wait_ge(l3["m"], l3.at("m", q.g))
                    V.tensor_tensor_scan(f(M[:]), f(w["hraw"][:]), f(w["ms"][:]), -BIG if first else Mb[:, R - 1, D - 1:D],
                                         ALU.add, ALU.max).then_inc(l3["m"], 1)
                    dve.wait_ge(l3["m"], l3.at("m", n))
                    ge(dve, l3["c"], l3.at("c", n - 1))
                    if first:
                        V.memset(w["xh2"][:, 0, 0:1], -BIG).then_inc(l3["carry"], 1)
                    else:
                        V.tensor_copy(w["xh2"][:, 0, 0:1], Mb[:, R - 1, D - 1:D]).then_inc(l3["carry"], 1)
                    dve.wait_ge(l3["carry"], l3.at("carry", n))
                    V.tensor_tensor(f(w["xhs"][:])[:, 1:G], f(w["hraw"][:])[:, 1:G], f(M[:])[:, 0:G - 1], ALU.add)
                    V.tensor_tensor(f(w["xhs"][:])[:, 0:1], f(w["hraw"][:])[:, 0:1], f(w["xh2"][:])[:, 0:1], ALU.add).then_inc(l3["e1"], 1)
                    dve.wait_ge(l3["e1"], l3.at("e1", n))
                    V.tensor_tensor(f(w["x1"][:]), f(w["xhs"][:]), f(M[:]), ALU.subtract).then_inc(l3["e2"], 1)
                    V.tensor_tensor(f(w["xh2"][:]), f(w["ms"][:]), f(M[:]), ALU.subtract).then_inc(l3["lm"], 1)
                    dve.wait_ge(l3["p"], l3.at("p", n))
                    dve.wait_ge(l3["mv"], l3.at("mv", n))
                    V.scalar_tensor_tensor(out=f(s2b[:, 0]), in0=pm3[0][:], scalar=col["bv"], in1=f(w["xc"][:]),
                                           op0=ALU.add, op1=ALU.mult).then_inc(l3["num"], 1)
                    dve.wait_ge(l3["c"], l3.at("c", n))
                    num, numb = (H[:, R * b:R * (b + 1), :] for b in (q.b, 1 - q.b))
                    den, denb = xin[:, q.b], xin[:, 1 - q.b]
                    dve.wait_ge(l3["num"], l3.at("num", n))
                    V.tensor_tensor_scan(f(num), f(w["xb"][:]), f(s2b[:, 0]), 0.0 if first else numb[:, R - 1, D - 1:D],
                                         ALU.mult, ALU.add).then_inc(l3["nsc"], 1)
                    V.tensor_tensor_scan(f(den), f(w["xb"][:]), f(w["xc"][:]), 0.0 if first else denb[:, R - 1, D - 1:D],
                                         ALU.mult, ALU.add).then_inc(l3["den"], 1)
                    dve.wait_ge(l3["den"], l3.at("den", n))
                    V.reciprocal(f(s2b[:, 1]), f(den)).then_inc(l3["rc"], 1)
                    dve.wait_ge(l3["rc"], l3.at("rc", n))
                    ge(dve, l3["mm"], l3.at("mm", n - 1))
                    V.tensor_tensor(f(w["ma"][:]), f(num), f(s2b[:, 1]), ALU.mult).then_inc(l3["o"], 1)
                    V.tensor_tensor(gT[:, 0, :].rearrange("p (r d) -> p r d", r=R), at[:, q.b],
                                    bcast(bsr), ALU.add).then_inc(l3["xb"], 1)
                    dve.wait_ge(l3["mm"], l3.at("mm", n))
                    dve.wait_ge(l3["xb"], l3.at("xb", n))
                    V.tensor_tensor(f(ub[:, q.b]), pm4[:], gT[:, 0, :], ALU.add).then_inc(l3["z"], 1)
                    dve.wait_ge(l3["z"], l3.at("z", n))
                    stats(lambda r: ub[:, q.b, r, :], 1, l3["var"], n)
                    variance(vin2[:], 1).then_inc(l3["var"], 1)
            edge_groups(V.Fori, l3_step)


_INS = ["x", "src", "dst", "edge_attr_128", "L0_gnn_g1", "L0_gnn_b1", "L0_gnn_g2", "L0_gnn_b2", "L0_gnn_eps_gin",
        "L0_gnn_Wg1", "L0_gnn_bg1", "L0_gnn_Wg2", "L0_gnn_bg2", "L0_gnn_Wf1", "L0_gnn_bf1", "L0_gnn_Wf2",
        "L0_gnn_bf2", "L1_gnn_eps", "L2_gnn_eps", "L2_gnn_W1", "L2_gnn_b1", "L2_gnn_gamma", "L2_gnn_beta",
        "L2_gnn_W2", "L2_gnn_b2", "L3_gnn_Wq", "L3_gnn_bq", "L3_gnn_Wk", "L3_gnn_bk", "L3_gnn_Wv", "L3_gnn_bv",
        "L3_gnn_Wskip", "L3_gnn_bskip"]


def kernel(**inputs):
    import numpy as _np
    import concourse.bacc as _bacc
    from concourse import mybir as _mybir
    from concourse.bass_utils import run_bass_kernel_spmd as _run

    nc = _bacc.Bacc("TRN2", target_bir_lowering=False, num_devices=1)
    arrays, args = {}, {}
    for name in _INS:
        v = _np.ascontiguousarray(inputs[name])
        v = v.reshape(v.shape or (1,))
        arrays[f"in_{name}_dram"] = v
        args[name] = nc.dram_tensor(f"in_{name}_dram", v.shape, _mybir.dt.from_np(v.dtype), kind="ExternalInput").ap()
    args["out"] = nc.dram_tensor("out_dram", (N, D), F32, kind="ExternalOutput").ap()
    build(nc, args)
    r = _run(nc, [arrays], core_ids=[0])
    return r.results[0]["out_dram"]
```

```python
from contextlib import ExitStack

import concourse.bass as bass
from concourse import mybir

F32 = mybir.dt.float32
I32 = mybir.dt.int32
U8 = mybir.dt.uint8
ALU = mybir.AluOpType
ACT = mybir.ActivationFunctionType

P = 128
N = 50000
E = 12500
D = 128
DF = 4 * D
R = 4
G = P * R
NG = -(-N // G)
LAST = N - G
SEEN = (NG - 1) * G - LAST
EG = 25
EP = EG * G
ET = EG * R
FAR = 65536
LN_EPS = 1e-5
BN_EPS = 1e-5
SM_SCALE = float(D) ** -0.5
BIG = 1e30
MAP_P = 80
PC = 5
KC = 2 * EG
KW = EP // KC
PIPE = NG + EG
MAP_PUT, MAP_GET, PRE_GOT = 2, 12, 24
MAP_PAIRS = ET // PC // 2


class Group:

    def __init__(self, i, b, kind):
        self.i, self.b, self.kind = i, b, kind
        self.g = 2 * i + b
        self.n = self.g + 1
        self.j = self.g - NG


def node_row(q):
    if isinstance(q.i, int) and q.g == NG - 1:
        return LAST
    return q.g * G


def build(nc, a):
    ctx = ExitStack()
    with ctx:
        def sb(name, shape, dt=F32):
            return ctx.enter_context(nc.sbuf_tensor(name, shape, dt))

        def pb(name, shape=(P, G)):
            return ctx.enter_context(nc.psum_tensor(name, list(shape), F32))

        def sem(name):
            return ctx.enter_context(nc.semaphore(name))

        def pair(name):
            return [sem(name + "0"), sem(name + "1")]

        def f(t):
            return t.rearrange("p r d -> p (r d)")

        xA = nc.dram_tensor("table_a", (N + EP, D), F32).ap()
        Y = nc.dram_tensor("table_y", (N + G, D), F32).ap()
        xB = nc.dram_tensor("table_b", (N, D), F32).ap()
        xC = nc.dram_tensor("table_c", (N + EP, D), F32).ap()
        xC_edges = nc.dram_tensor("table_c_edges", (EP, D), F32).ap()
        newest = nc.dram_tensor("newest", (N, 1), I32).ap()
        dst_tab = nc.dram_tensor("dst_sorted", (EP + 2,), I32).ap()
        src_tab = nc.dram_tensor("src_sorted", (EP,), I32).ap()
        perm_tab = nc.dram_tensor("edge_order", (EP,), I32).ap()

        ident = sb("ident", [P, P])
        ones = sb("ones", [P, P])
        mhalf = sb("mhalf", [P, 8])
        fresh = sb("fresh", [P, 1])
        Wg1, Wg2 = sb("Wg1", [P, D]), sb("Wg2", [P, D])
        Wf1, Wf2 = sb("Wf1", [P, DF]), sb("Wf2", [P, 4, D])
        Wq, Wk, Wv, Ws = sb("Wq", [P, D]), sb("Wk", [P, D]), sb("Wv", [P, D]), sb("Wskip", [P, D])
        W1, W2 = sb("W1", [P, D]), sb("W2", [P, D])
        W1T, W2T = sb("W1T", [P, D]), sb("W2T", [P, D])
        bg2r, bf2r, b2r, bsr = sb("bg2r", [P, D]), sb("bf2r", [P, D]), sb("b2r", [P, D]), sb("bsr", [P, D])
        COLS = ["g1", "b1", "g2", "b2", "bg1", "L2b1", "gamma", "beta", "bq", "bk", "bv"]
        cols = sb("cols", [P, len(COLS)])
        col = {n: cols[:, k:k + 1] for k, n in enumerate(COLS)}
        bf1c = sb("bf1c", [P, 4])
        eps3 = sb("eps3", [P, 3])
        k1 = sb("k1", [P, 5])
        one_eg, g1s, b1s, two_e1, one_e2 = (k1[:, k:k + 1] for k in range(5))
        rows_i = sb("rows_i", [ET, 4, P], I32)
        rows_f = sb("rows_f", [ET, 8, P])
        skip_or_dst = sb("skip_or_dst", [P, ET], I32)
        dst_i = sb("dst_i", [P, ET], I32)
        src_i = sb("src_i", [P, ET], I32)
        perm_i = sb("perm_i", [P, ET], I32)
        pos_i = sb("pos_i", [P, ET], I32)
        news_i = sb("news_i", [P, ET], I32)
        newd_i = sb("newd_i", [P, ET], I32)
        newd_edge = dst_i
        src_f = sb("src_f", [P, ET])
        spare = sb("spare", [P, R])
        open_rows = sb("open_rows", [P, NG, R])
        is_last = sb("is_last", [P, ET])
        keep = sb("keep", [P, EP], U8)
        ixr = sb("ixr", [P, 2, 8], I32)
        ixs = sb("ixs", [P, 2, 8], I32)
        newr = sb("newr", [P, 2, 16], I32)
        X = sb("X", [P, ET, D])
        H = sb("H", [P, ET, D])
        HT = H[:].rearrange("p t d -> p (t d)")
        xin = sb("xin", [P, 2, R, D])
        gr = sb("gr", [P, 2, R, D])
        at = sb("at", [P, 2, R, D])
        w = {n: sb("w_" + n, [P, R, D]) for n in ("xh1", "h", "r", "xb", "xc", "x1", "xh2", "n2",
                                                  "xhs", "hraw", "ms", "ma", "msg", "f0", "f1")}
        gm = sb("gm", [P, R, D + 1])
        gms = [gm, None]
        s2b = sb("s2b", [P, 2, R, D])
        gT = sb("gT", [P, 4, G])
        gms[1] = gT[:].rearrange("p c g -> p (c g)")[:, 0:R * (D + 1)].rearrange("p (r d) -> p r d", r=R)
        ub = sb("ub", [P, 2, R, D])
        oA = sb("oA", [P, 2, R, D])
        oB = sb("oB", [P, 2, R, D])
        stt = sb("stt", [P, 4, R, 6])
        mv = sb("mv", [P, 4, R, 2])
        vinc, vin2, vin3 = sb("vinc", [P, 8]), sb("vin2", [P, R]), sb("vin3", [P, R])
        vin_nb = (vin2, vin3)
        nma, nmb, rb = sb("nma", [P, R]), sb("nmb", [P, R]), sb("rb", [P, R])
        mbig = sb("mbig", [P, 1])
        zero_row = sb("zero_row", [P, D + 1])
        order_rows = sb("order_rows", [ET, P], I32)
        ro = sb("ro", [P, 8])
        r2 = sb("r2", [P, R])
        r3 = sb("r3", [P, 2, R])
        sm = sb("sm", [P, 8, R])
        keys = at[:].rearrange("p b r d -> p b (r d)").bitcast(I32)
        put_at = sb("put_at", [P, 2, R], I32)
        sums_at = sb("sums_at", [P, 2, R], I32)
        spare_i = sb("spare_i", [P, R], I32)
        cov = sb("cov", [P, D + 1])
        covE = sb("covE", [P, D + 1])
        bn = sb("bn", [P, 12])
        bn_a, bn_b = bn[:, 9:10], bn[:, 10:11]
        later_mask = HT[:, 0:R * G].rearrange("p (r g) -> p r g", r=R)
        l1_junk = [t[:, b].rearrange("p r d -> p (r d)") for t in (oB, ub) for b in range(2)]
        open_i = f(w["xhs"][:]).bitcast(I32)[:, 0:NG * R].rearrange("p (g r) -> p g r", g=NG)
        nums, bases, dens = ([H[:, R * (2 * k + b):R * (2 * k + b + 1), :] for b in range(2)] for k in range(3))
        own_row = HT[0:MAP_P, 0:N // MAP_P].bitcast(I32)
        dst_row = [at[:, b].rearrange("p r d -> p (r d)").bitcast(I32)[:, 0:KW + 1] for b in range(2)]
        pT1, pT2, pm1, pm2, pm4, pG = (pb(x) for x in ("pT1", "pT2", "pm1", "pm2", "pm4", "pG"))
        pm3 = [pb("pm3a"), pb("pm3b")]

        def rows4(ap):
            return ap.rearrange("(p r) d -> p r d", r=R)

        def store_rows(sp, table, q, buf):
            if isinstance(q.i, int) and q.g == NG - 1:
                return sp.dma_start(rows4(table[LAST + SEEN:N, :]), buf[SEEN // R:P])
            return sp.dma_start(rows4(table[span(q.g * G, G), :]), buf)

        def edge4(ap):
            return ap.rearrange("(r p) d -> p r d", p=P)

        def span(start, size):
            return slice(start, start + size) if isinstance(start, int) else bass.ds(start, size)

        def ge(eng, s, v):
            if not (isinstance(v, int) and v <= 0):
                eng.wait_ge(s, v)

        def after_wait(eng):
            eng.sem_inc(waited, 1)

        def bcast(t):
            return t[:].unsqueeze(1).to_broadcast([P, R, D])

        const_loaded = sem("const_loaded")
        waited = sem("waited")
        pool_const = sem("pool_const")
        tables_written = sem("tables_written")
        setup_dve = sem("setup_dve")
        setup_pe = sem("setup_pe")
        dst_row_loaded = pair("dst_row_loaded")
        keep_made = sem("keep_made")

        def const_dmas():
            for t, k in ((Wg1, "L0_gnn_Wg1"), (Wg2, "L0_gnn_Wg2"), (Wf1, "L0_gnn_Wf1"), (Wq, "L3_gnn_Wq"),
                         (Wk, "L3_gnn_Wk"), (Wv, "L3_gnn_Wv"), (Ws, "L3_gnn_Wskip"), (W1, "L2_gnn_W1"),
                         (W2, "L2_gnn_W2")):
                yield t[:], a[k]
            yield Wf2[:], a["L0_gnn_Wf2"].rearrange("(c p) d -> p c d", p=P)
            for c in range(4):
                yield bf1c[:, c:c + 1], a["L0_gnn_bf1"][c * P:(c + 1) * P].rearrange("(p o) -> p o", o=1)
            for n, k in zip(COLS, ("L0_gnn_g1", "L0_gnn_b1", "L0_gnn_g2", "L0_gnn_b2", "L0_gnn_bg1",
                                   "L2_gnn_b1", "L2_gnn_gamma", "L2_gnn_beta", "L3_gnn_bq", "L3_gnn_bk",
                                   "L3_gnn_bv")):
                yield col[n], a[k].rearrange("(p o) -> p o", o=1)
            for t, k in ((bg2r, "L0_gnn_bg2"), (bf2r, "L0_gnn_bf2"), (b2r, "L2_gnn_b2"), (bsr, "L3_gnn_bskip")):
                yield t[:], a[k].partition_broadcast(P)
            for c, k in enumerate(("L0_gnn_eps_gin", "L1_gnn_eps", "L2_gnn_eps")):
                yield eps3[:, c:c + 1], a[k].partition_broadcast(P)

        CONST = 16 * len(list(const_dmas()))
        POOL_CONST, ROWS_READY, SETUP_DVE = 15, 16, 24
        BN_COV, BN_QUAD, BN_VAR, BN_DONE = 5, 7, 11, 1

        def run_pipeline(fori, step):
            def peeled(first, end):
                for s in range(first, end):
                    at_stage = [Group((s - lag) // 2, (s - lag) % 2, "N" if s - lag < NG else "E")
                                if 0 <= s - lag < PIPE else None for lag in range(5)]
                    step(s // 2, s % 2, *at_stage)

            def looped(first, end, kind, work=None):
                if work is not None or kind == "E":
                    for k in range(2):
                        step(first, k, *(Group(first + (k - lag) // 2, (k - lag) % 2, kind) for lag in range(5)),
                             work=work)
                    first += 1
                with fori(first, end) as i:
                    for k in range(2):
                        step(i, k, *(Group(i + (k - lag) // 2, (k - lag) % 2, kind) for lag in range(5)),
                             work=work)

            peeled(0, 2 * MAP_PUT)
            looped(MAP_PUT, MAP_GET, "N", "put")
            looped(MAP_GET, MAP_GET + MAP_PAIRS, "N", "get")
            looped(MAP_GET + MAP_PAIRS, PRE_GOT, "N")
            looped(PRE_GOT, NG // 2 - 1, "N", "pre")
            for s in (NG - 2, NG - 1):
                step(s // 2, s % 2, *(Group((s - lag) // 2, (s - lag) % 2, "N") for lag in range(5)), work="pre")
            peeled(NG, NG + 4)
            looped((NG + 4) // 2, (PIPE - 1) // 2, "E")
            peeled(PIPE - 1, PIPE + 4)

        def passes(fori, kind, lags, step):
            count = NG if kind == "N" else EG

            def peeled(first, end):
                for s in range(first, end):
                    step(*(Group((s - lag) // 2, (s - lag) % 2, kind) if 0 <= s - lag < count else None
                           for lag in range(lags + 1)))

            first, last = (lags + 1) // 2 + 1, (count - 1) // 2
            peeled(0, 2 * first)
            with fori(first, last) as i:
                for k in range(2):
                    step(*(Group(i + (k - lag) // 2, (k - lag) % 2, kind) for lag in range(lags + 1)))
            peeled(2 * last, count + lags)

        def batch_pass(fori, step):
            def group(i, k):
                q = Group(i, k % 2, "N")
                q.rows = (xin, at)[k // 2 % 2][:, q.b]
                return q

            def peeled(first, end):
                for s in range(first, end):
                    step(*(group((s - lag) // 2, (s - lag) % 4) if 0 <= s - lag < NG else None for lag in (-1, 0, 2)))

            peeled(0, 4)
            with fori(1, NG // 4) as i:
                for k in range(4):
                    step(*(group(i * 2 + (k - lag) // 2, (k - lag) % 4) for lag in (-1, 0, 2)))
            peeled(NG // 4 * 4, NG + 2)

        def edge_groups(fori, step):
            passes(fori, "E", 1, step)

        def node_passes(fori, step):
            def peeled(first, end):
                for s in range(first, end):
                    step(*(Group((s - lag) // 2, (s - lag) % 2, "N") if 0 <= s - lag < NG else None
                           for lag in range(5)))

            def looped(first, last, own):
                with fori(first, last) as i:
                    for k in range(2):
                        qs = [Group(i + (k - lag) // 2, (k - lag) % 2, "N") for lag in range(5)]
                        qs[0].own = own
                        step(*qs)
            peeled(0, 6)
            looped(3, EG, True)
            looped(EG, NG // 2 - 1, False)
            peeled(NG - 2, NG + 4)

        def own_pair(p):
            return p.i < EG if isinstance(p.i, int) else p.own

        def tile(ap, q, r):
            return ap[:, span(q * R + r, 1), :].rearrange("p o d -> p (o d)")

        x_loaded = pair("x_loaded")
        attr_got = pair("attr_got")
        var = {n: sem("var_" + n) for n in "123s"}
        nma_made, nmb_made = sem("nma_made"), sem("nmb_made")
        powc, pow2, pow3 = sem("powc"), sem("pow2"), sem("pow3")
        xb_made, xc_made, s_made = sem("xb_made"), sem("xc_made"), sem("s_made")
        xh1_made, xh2_made, xhs_made = sem("xh1_made"), sem("xh2_made"), sem("xhs_made")
        x1_made, u_made = sem("x1_made"), sem("u_made")
        t1_done, t2_done, ts_done, ta_done = sem("t1_done"), sem("t2_done"), sem("ts_done"), sem("ta_done")
        h_made, hraw_made, he_made, n2_made = sem("h_made"), sem("hraw_made"), sem("he_made"), sem("n2_made")
        mm1_done, mm2_done, mm3_done, mm4_done = sem("mm1_done"), sem("mm2_done"), sem("mm3_done"), sem("mm4_done")
        r_made, gelu_made = sem("r_made"), sem("gelu_made")
        xA_made, y_made = sem("xA_made"), sem("y_made")
        xA_stored, y_stored = pair("xA_stored"), pair("y_stored")
        y_put, open_loaded = pair("y_put"), sem("open_loaded")
        xAe_stored = pair("xAe_stored")
        ms_made, ma_made, msg_made, agg_made = sem("ms_made"), sem("ma_made"), sem("msg_made"), sem("agg_made")
        map_put, map_got, new_kept = pair("map_put"), pair("map_got"), pair("new_kept")
        ix_put, ix_got, ix_attr = sem("ix_put"), sem("ix_got"), sem("ix_attr")
        pre_got, pre_kept = pair("pre_got"), pair("pre_kept")

        class Steps:

            def __init__(self, prefix, *chains):
                self.where = {}
                for chain in chains:
                    names = chain.split()
                    s = sem(prefix + names[0])
                    for k, name in enumerate(names):
                        self.where[name] = s, k + 1, len(names)

            def __getitem__(self, name):
                return self.where[name][0]

            def at(self, name, n):
                _, k, total = self.where[name]
                return total * (n - 1) + k if total > 1 else n

        l1 = Steps("l1_", "ix", "same count far dup away mul idx", "sum", "rows")
        l1_got, l1_added, l1_keys = pair("l1_got"), pair("l1_added"), pair("l1_keys")
        nb = Steps("nb_", "var", "pw", "x", "m", "gram")
        nb_loaded, nb_stored = pair("nb_loaded"), pair("nb_stored")
        l2 = Steps("l2_", "ix", "t tb", "tg gram mm", "scan g", "gm gt h", "x")
        l2_got, l2_own = pair("l2_got"), pair("l2_own")
        bns = Steps("bn_", "dve", "pe", "pw", "ready")
        q2 = Steps("q2_", "r", "rt", "mm", "y", "var", "pw", "x")
        q2_stored = pair("q2_stored")
        n2 = Steps("n2_", "ta mm1", "mm2", "tc mm3", "c r", "rt", "ct", "o", "nm", "xc", "z", "var2",
                   "y", "var", "x2", "xcb", "pw", "pw2")
        n2_loaded, n2_cst, n2_ost = pair("n2_loaded"), pair("n2_cst"), pair("n2_ost")
        l3 = Steps("l3_", "ix", "ts td mq mk mm ml mv", "tn", "cp xs xd q", "pen l c p", "qk base",
                   "m carry e1 e2 lm num nsc den", "rc z", "var", "pw", "out")
        l3_got, l3_put, l3_ix_put = pair("l3_got"), pair("l3_put"), sem("l3_ix_put")
        own_got, own_kept, own_ix = sem("own_got"), sem("own_kept"), sem("own_ix")

        PAIRS_N = NG // 2

        block = ctx.enter_context(nc.Block())

        @block.sync
        def _(sp):
            for dst, src in const_dmas():
                sp.dma_start(dst, src).then_inc(const_loaded, 16)
            sp.wait_ge(pool_const, POOL_CONST)
            pad, zero = rows_i[0:1, 0:3, :].rearrange("a b c -> a (b c)"), rows_i[0:1, 3, :]
            sp.dma_start(dst_tab[0:1].unsqueeze(0), pad[:, 0:1]).then_inc(tables_written, 16)
            sp.dma_start(dst_tab[1:1 + E], a["dst"]).then_inc(tables_written, 16)
            sp.dma_start(dst_tab[1 + E:EP + 2].unsqueeze(0), pad[:, 0:EP + 1 - E]).then_inc(tables_written, 16)
            sp.dma_start(src_tab[0:E], a["src"]).then_inc(tables_written, 16)
            for c in range(3):
                sp.dma_start(src_tab[E + 100 * c:E + 100 * (c + 1)].unsqueeze(0),
                             zero[:, 0:100]).then_inc(tables_written, 16)
            sp.dma_start(perm_tab.rearrange("(t p) -> t p", p=P), order_rows[:]).then_inc(tables_written, 16)
            sp.dma_start(newest.rearrange("(p r) o -> p (r o)", p=MAP_P), own_row).then_inc(tables_written, 16)
            sp.wait_ge(tables_written, 16 * 9)
            sp.dma_start(edge4(Y[N:N + G, :]), oB[:, 0]).then_inc(tables_written, 16)
            for k, t in enumerate((dst_tab[1:1 + EP], dst_tab[2:2 + EP], src_tab, perm_tab)):
                sp.dma_start(rows_i[:, k, :], t.rearrange("(t p) -> t p", p=P)).then_inc(tables_written, 16)

            def load(q):
                ge(sp, xh1_made, q.n - 2)
                ge(sp, xb_made, q.n - 2)
                ge(sp, xc_made, q.n - 2)
                sp.dma_start(xin[:, q.b], rows4(a["x"][span(node_row(q), G), :])).then_inc(x_loaded[q.b], 16)

            def step(i, k, fr, mi, ba, ta, od, work=None):
                if work == "pre":
                    c = 2 * (i - PRE_GOT) + k
                    ge(sp, keep_made, c - 1)
                    after_wait(sp)
                    sp.dma_start(dst_row[k], dst_tab[span(c * KW, KW + 1)].partition_broadcast(P)).then_inc(dst_row_loaded[k], 16)
                if fr is not None and fr.kind == "N" and not (isinstance(fr.i, int) and fr.g == NG - 1):
                    load(Group(fr.i + (fr.b + 1) // 2, 1 - fr.b, "N"))
                if ta is not None:
                    sp.wait_ge(xA_made, ta.n)
                    if ta.kind == "N":
                        store_rows(sp, xA, ta, oA[:, ta.b]).then_inc(xA_stored[ta.b], 16)
                        sp.wait_ge(y_made, ta.n)
                        store_rows(sp, Y, ta, oB[:, ta.b]).then_inc(y_stored[ta.b], 16)
                    else:
                        sp.dma_start(edge4(xA[span(N + ta.j * G, G), :]), X[:, span(ta.j * R, R), :]).then_inc(xAe_stored[ta.b], 16)
                if work == "get":
                    c = 2 * (i - MAP_GET) + k
                    sp.wait_ge(map_got[k], 32 * PC * (i - MAP_GET + 1))
                    sp.dma_start(news_i[:, span(c * PC, PC)], newr[:, k, 0:PC]).then_inc(new_kept[k], 16)
                    sp.dma_start(newd_i[:, span(c * PC, PC)], newr[:, k, 8:8 + PC]).then_inc(new_kept[k], 16)
                if work == "pre":
                    sp.wait_ge(pre_got[k], 16 * R * (i - PRE_GOT + 1))
                    after_wait(sp)
                    sp.dma_start((X if k else H)[:, span((i - PRE_GOT) * R, R), :], gr[:, k]).then_inc(pre_kept[k], 16)

            load(Group(0, 0, "N"))
            run_pipeline(nc.sync.Fori, step)

            sp.wait_ge(ts_done, EG)
            for b in range(2):
                sp.wait_ge(map_put[b], 16 * PC * MAP_PAIRS)

            def l1_step(q, _):
                if q is not None:
                    ge(sp, l1["same"], l1.at("same", q.n - 2))
                    sp.dma_start(keys[:, q.b], src_tab[span(q.g * G, G)].partition_broadcast(P)).then_inc(l1_keys[q.b], 16)
                    for k in range(4):
                        if isinstance(q.i, int) and 4 * q.g + k >= NG:
                            continue
                        row = LAST if isinstance(q.i, int) and 4 * q.g + k == NG - 1 else (4 * q.g + k) * G
                        sp.dma_start(open_i[:, span(4 * q.g + k, 1), :].rearrange("p o r -> p (o r)"),
                                     newest[span(row, G), :].rearrange("(p r) o -> p (r o)", r=R)).then_inc(open_loaded, 16)
            edge_groups(nc.sync.Fori, l1_step)

            for b in range(2):
                sp.wait_ge(l1_added[b], 16 * R * ((EG + 1 - b) // 2))

            def nb_load(p):
                ge(sp, nb["var"], 3 * (p.n - 2))
                after_wait(sp)
                ge(sp, nb["x"], nb.at("x", p.n - 4))
                after_wait(sp)
                sp.dma_start(p.rows, rows4(Y[span(node_row(p), G), :])).then_inc(nb_loaded[p.b], 16)

            def nb_step(coming, p, before):
                if p is not None and isinstance(p.i, int) and p.g == 0:
                    nb_load(p)
                if coming is not None:
                    nb_load(coming)
                if before is not None:
                    sp.wait_ge(nb["x"], nb.at("x", before.n))
                    store_rows(sp, xB, before, oA[:, before.b]).then_inc(nb_stored[before.b], 16)
            batch_pass(nc.sync.Fori, nb_step)

            def q2_store(q, _):
                if q is not None:
                    sp.wait_ge(q2["x"], q2.at("x", q.n))
                    sp.dma_start(edge4(xC[span(N + q.g * G, G), :]), X[:, span(q.g * R, R), :]).then_inc(q2_stored[q.b], 16)
                    sp.dma_start(edge4(xC_edges[span(q.g * G, G), :]), X[:, span(q.g * R, R), :]).then_inc(q2_stored[q.b], 16)
            edge_groups(nc.sync.Fori, q2_store)

            def n2_load(p):
                ge(sp, n2["ta"], n2.at("ta", p.n - 2))
                after_wait(sp)
                ge(sp, n2["x2"], n2.at("x2", p.n - 2))
                after_wait(sp)
                sp.dma_start(xin[:, p.b], rows4(xB[span(node_row(p), G), :])).then_inc(n2_loaded[p.b], 16)

            def n2_step(p, mi, ba, ta, la):
                if p is not None and not (isinstance(p.i, int) and p.g == NG - 1):
                    n2_load(Group(p.i + (p.b + 1) // 2, 1 - p.b, "N"))
                if ba is not None:
                    sp.wait_ge(n2["xc"], n2.at("xc", ba.n))
                    store_rows(sp, xC, ba, oA[:, ba.b]).then_inc(n2_cst[ba.b], 16)
                if la is not None:
                    sp.wait_ge(n2["o"], n2.at("o", la.n))
                    store_rows(sp, a["out"], la, s2b[:, la.b]).then_inc(n2_ost[la.b], 16)
                if p is not None and p.b == 1 and own_pair(p):
                    sp.wait_ge(own_got, 16 * R * (p.i + 1))
                    after_wait(sp)
                    sp.dma_start(X[:, span(p.i * R, R), :], gr[:, 0]).then_inc(own_kept, 16)
            n2_load(Group(0, 0, "N"))
            node_passes(nc.sync.Fori, n2_step)
            for b in range(2):
                sp.wait_ge(n2_ost[b], 16 * PAIRS_N)
                sp.wait_ge(l3_put[b], 16 * R * ((EG + 1 - b) // 2))

        @block.gpsimd
        def _(pool):
            POOL = nc.gpsimd
            POOL.memset(gm[:], 0.0).then_inc(pool_const, 1)
            POOL.memset(ident[:], 0.0).then_inc(pool_const, 1)
            POOL.memset(ones[:], 1.0).then_inc(pool_const, 1)
            POOL.memset(mhalf[:], -0.5).then_inc(pool_const, 1)
            POOL.memset(vinc[:], 1.0).then_inc(pool_const, 1)
            POOL.memset(oB[:], 0.0).then_inc(pool_const, 1)
            POOL.iota(spare_i[:], [[P, R]], base=N, channel_multiplier=1).then_inc(pool_const, 1)
            POOL.memset(rows_i[:, 0:3, :], FAR - 1).then_inc(pool_const, 1)
            POOL.memset(rows_i[:, 3, :], FAR - 1).then_inc(pool_const, 1)
            POOL.memset(fresh[:], 1.0).then_inc(pool_const, 1)
            POOL.iota(order_rows[:], [[1, P]], base=0, channel_multiplier=P).then_inc(pool_const, 1)
            POOL.iota(own_row, [[1, N // MAP_P]], base=0, channel_multiplier=N // MAP_P).then_inc(pool_const, 1)
            POOL.iota(pos_i[:], [[P, ET]], base=N, channel_multiplier=1).then_inc(pool_const, 1)
            pool.wait_ge(pool_const, 13)
            POOL.affine_select(out=ident[:], in_=ident[:], compare_op=ALU.not_equal, fill=1.0, base=0,
                               pattern=[[-1, P]], channel_multiplier=1).then_inc(pool_const, 1)
            POOL.affine_select(out=fresh[:], in_=fresh[:], compare_op=ALU.is_ge, fill=0.0, base=-(SEEN // R),
                               pattern=[[0, 1]], channel_multiplier=1).then_inc(pool_const, 1)
            pool.wait_ge(const_loaded, CONST)
            pool.wait_ge(setup_dve, SETUP_DVE)

            def inverse_root(out, in_):
                return POOL.tensor_tensor(out, in_, mhalf[:, 0:in_.shape[-1]], ALU.pow)

            def gather(dst, table, index, s):
                POOL.indirect_dma_start(dst, None, table, bass.IndirectOffsetOnAxis(ap=index, axis=0)).then_inc(s, 16)

            def indices(ring, lst, t, count, s, n):
                POOL.tensor_copy(ring[:, 0:count], lst[:, span(t, count)]).then_inc(s, 1)
                pool.wait_ge(s, n)
                after_wait(pool)

            def attr_gather(j, i, b):
                ge(pool, ta_done, j - 1)
                indices(ixr[:, b], perm_i, j * R, R, ix_attr, j + 1)
                for r in range(R):
                    gather(at[:, b, r, :], a["edge_attr_128"], ixr[:, b, r:r + 1], attr_got[b])

            def map_scatter(k, t):
                POOL.indirect_dma_start(newest, bass.IndirectOffsetOnAxis(ap=ixr[:, k, t:t + 1], axis=0),
                                        ixs[:, k, t:t + 1], None, bounds_check=N - 1,
                                        oob_is_err=False).then_inc(map_put[k], 16)

            def map_gather(k, t):
                gather(newr[:, k, t:t + 1], newest, ixr[:, k, t:t + 1], map_got[k])
                gather(newr[:, k, 8 + t:9 + t], newest, ixs[:, k, t:t + 1], map_got[k])

            def step(i, k, fr, mi, ba, ta, od, work=None):
                if fr is not None:
                    pool.wait_ge(var["1"], 3 * fr.n)
                    if fr.kind == "E":
                        pool.wait_ge(var["s"], 3 * (fr.j + 1))
                        ge(pool, xhs_made, fr.j)
                    ge(pool, xh1_made, fr.n - 1)
                    inverse_root(ro[:, 0:8 if fr.kind == "E" else 4], vinc[:, 0:8 if fr.kind == "E" else 4]).then_inc(powc, 1)
                if work == "put":
                    c = 2 * (i - MAP_PUT) + k
                    ge(pool, map_put[k], 16 * PC * (i - MAP_PUT))
                    indices(ixr[:, k], skip_or_dst, c * PC, PC, ix_put, 2 * c + 1)
                    indices(ixs[:, k], pos_i, c * PC, PC, ix_put, 2 * c + 2)
                    for t in range(2):
                        map_scatter(k, t)
                if work == "get":
                    c = 2 * (i - MAP_GET) + k
                    for b in range(2):
                        pool.wait_ge(map_put[b], 16 * PC * MAP_PAIRS)
                    ge(pool, new_kept[k], 32 * (i - MAP_GET))
                    indices(ixr[:, k], src_i, c * PC, PC, ix_got, 2 * c + 1)
                    indices(ixs[:, k], dst_i, c * PC, PC, ix_got, 2 * c + 2)
                    for t in range(2):
                        map_gather(k, t)
                if work == "pre":
                    ge(pool, pre_kept[k], 16 * (i - PRE_GOT))
                    indices(ixr[:, k], dst_i if k else src_i, (i - PRE_GOT) * R, R, ix_got,
                            4 * MAP_PAIRS + 2 * (i - PRE_GOT) + k + 1)
                    for r in range(2):
                        gather(gr[:, k, r, :], a["x"], ixr[:, k, r:r + 1], pre_got[k])
                if mi is not None:
                    pool.wait_ge(var["2"], 3 * mi.n)
                    ge(pool, xh2_made, mi.n - 1)
                    inverse_root(r2[:], vin2[:]).then_inc(pow2, 1)
                if work == "put":
                    for t in range(2, PC):
                        map_scatter(k, t)
                if work == "get":
                    for t in range(2, PC):
                        map_gather(k, t)
                if work == "pre":
                    for r in range(2, R):
                        gather(gr[:, k, r, :], a["x"], ixr[:, k, r:r + 1], pre_got[k])
                if fr is not None and fr.kind == "E":
                    if isinstance(fr.i, int) and fr.j == 0:
                        attr_gather(0, NG // 2, 0)
                    if not (isinstance(fr.i, int) and fr.j == EG - 1):
                        attr_gather(fr.j + 1, fr.i + (fr.b + 1) // 2, 1 - fr.b)
                if ta is not None and ta.kind == "E":
                    for b in range(2):
                        pool.wait_ge(y_stored[b], 16 * PAIRS_N)
                    ge(pool, y_put[ta.b], 16 * R * (ta.i - NG // 2))
                    indices(ixs[:, ta.b], skip_or_dst, ta.j * R, R, ix_put, 2 * 2 * MAP_PAIRS + ta.j + 1)
                    pool.wait_ge(y_made, ta.n)
                    after_wait(pool)
                    for r in range(R):
                        POOL.indirect_dma_start(Y, bass.IndirectOffsetOnAxis(ap=ixs[:, ta.b, r:r + 1], axis=0),
                                                oB[:, ta.b, r, :], None, bounds_check=N - 1,
                                                oob_is_err=False).then_inc(y_put[ta.b], 16)
                if ba is not None:
                    pool.wait_ge(var["3"], 3 * ba.n)
                    ge(pool, xA_made, ba.n - 2)
                    ge(pool, y_made, ba.n - 2)
                    inverse_root(r3[:, ba.b], vin3[:]).then_inc(pow3, 1)

            run_pipeline(POOL.Fori, step)

            pool.wait_ge(xhs_made, EG)
            POOL.memset(later_mask, 1.0).then_inc(pool_const, 1)
            pool.wait_ge(pool_const, POOL_CONST + 1)
            POOL.affine_select(out=later_mask, in_=later_mask, compare_op=ALU.is_gt, fill=0.0, base=0,
                               pattern=[[-P, R], [1, G]], channel_multiplier=-1).then_inc(pool_const, 1)
            pool.wait_ge(tables_written, 16 * 14)
            for b in range(2):
                pool.wait_ge(xA_stored[b], 16 * PAIRS_N)
                pool.wait_ge(xAe_stored[b], 16 * ((EG + 1 - b) // 2))
                pool.wait_ge(new_kept[b], 32 * MAP_PAIRS)
                pool.wait_ge(y_put[b], 16 * R * ((EG + 1 - b) // 2))

            def l1_step(q, before):
                if q is not None:
                    ge(pool, l1["sum"], l1.at("sum", q.n - 2))
                    indices(ixr[:, q.b], newd_i, q.g * R, R, l1["ix"], q.n)
                    for r in range(R):
                        gather(gr[:, q.b, r, :], xA, ixr[:, q.b, r:r + 1], l1_got[q.b])
                if before is not None:
                    pool.wait_ge(l1["idx"], l1.at("idx", before.n))
                    pool.wait_ge(l1["rows"], l1.at("rows", before.n))
                    ge(pool, l1_added[1 - before.b], 16 * R * (before.i + before.b))
                    after_wait(pool)
                    for r in range(R):
                        POOL.indirect_dma_start(Y, bass.IndirectOffsetOnAxis(ap=sums_at[:, before.b, r:r + 1], axis=0),
                                                oA[:, before.b, r, :], None, bounds_check=N + G - 1,
                                                compute_op=ALU.add).then_inc(l1_added[before.b], 16)
            edge_groups(POOL.Fori, l1_step)

            def nb_step(coming, p, before):
                if p is not None:
                    pool.wait_ge(nb["var"], 3 * p.n)
                    ge(pool, nb["x"], nb.at("x", p.n - 2))
                    inverse_root(r3[:, p.b], vin_nb[p.b][:]).then_inc(nb["pw"], 1)
            batch_pass(POOL.Fori, nb_step)

            for b in range(2):
                pool.wait_ge(nb_stored[b], 16 * PAIRS_N)

            def l2_step(q, before):
                if q is not None:
                    ge(pool, l2["t"], l2.at("t", q.n - 2))
                    ge(pool, l2["g"], l2.at("g", q.n - 2))
                    ge(pool, l2["x"], l2.at("x", q.n - 2))
                    indices(ixr[:, q.b], src_i, q.g * R, R, l2["ix"], 2 * q.g + 1)
                    indices(ixs[:, q.b], dst_i, q.g * R, R, l2["ix"], 2 * q.g + 2)
                    for r in range(R):
                        gather(gr[:, q.b, r, :], xB, ixr[:, q.b, r:r + 1], l2_got[q.b])
                        gather(at[:, q.b, r, :], xB, ixs[:, q.b, r:r + 1], l2_own[q.b])
            edge_groups(POOL.Fori, l2_step)
            pool.wait_ge(bns["dve"], BN_VAR)
            inverse_root(bn[:, 5:6], bn[:, 4:5]).then_inc(bns["pw"], 1)

            def q2_step(q, mi, ba):
                if mi is not None:
                    pool.wait_ge(q2["var"], 3 * mi.n)
                    ge(pool, q2["x"], q2.at("x", mi.n - 1))
                    inverse_root(r2[:], vin2[:]).then_inc(q2["pw"], 1)
            passes(POOL.Fori, "E", 2, q2_step)
            pool.wait_ge(setup_dve, SETUP_DVE + 3)
            for b in range(2):
                pool.wait_ge(q2_stored[b], 32 * ((EG + 1 - b) // 2))

            def n2_step(p, mi, ba, ta, la):
                if p is not None:
                    pool.wait_ge(n2_loaded[p.b], 16 * (p.i + 1))
                    ge(pool, n2["y"], n2.at("y", p.n - 2))
                    POOL.tensor_tensor(at[:, p.b], xin[:, p.b], xin[:, p.b], ALU.add).then_inc(n2["x2"], 1)
                if ba is not None:
                    pool.wait_ge(n2["xc"], n2.at("xc", ba.n))
                    ge(pool, n2["z"], n2.at("z", ba.n - 1))
                    POOL.tensor_tensor(w["xb"][:], oA[:, ba.b], bcast(bsr), ALU.add).then_inc(n2["xcb"], 1)
                if ta is not None:
                    pool.wait_ge(n2["var2"], 3 * ta.n)
                    ge(pool, n2["o"], n2.at("o", ta.n - 2))
                    inverse_root(r3[:, ta.b], vin3[:]).then_inc(n2["pw2"], 1)
                if p is not None and own_pair(p):
                    if p.b == 0:
                        ge(pool, own_kept, 16 * p.i)
                        indices(ixr[:, 0], newd_edge, p.i * R, R, own_ix, p.i + 1)
                    for r in (2 * p.b, 2 * p.b + 1):
                        gather(gr[:, 0, r, :], xC_edges, ixr[:, 0, r:r + 1], own_got)
                if mi is not None:
                    pool.wait_ge(n2["var"], 3 * mi.n)
                    ge(pool, n2["xc"], n2.at("xc", mi.n - 1))
                    inverse_root(r2[:], vin2[:]).then_inc(n2["pw"], 1)
            node_passes(POOL.Fori, n2_step)

            for b in range(2):
                pool.wait_ge(n2_cst[b], 16 * PAIRS_N)
                pool.wait_ge(n2_ost[b], 16 * PAIRS_N)

            def l3_gather(q):
                ge(pool, l3["ts"], l3.at("ts", q.n - 2))
                indices(ixr[:, q.b], news_i, q.g * R, R, l3["ix"], q.n)
                for r in range(R):
                    gather(gr[:, q.b, r, :], xC, ixr[:, q.b, r:r + 1], l3_got[q.b])
            l3_gather(Group(0, 0, "E"))

            def l3_step(q, mi, ba, ta):
                if q is not None and not (isinstance(q.i, int) and q.g == EG - 1):
                    l3_gather(Group(q.i + (q.b + 1) // 2, 1 - q.b, "E"))
                if ta is not None:
                    pool.wait_ge(l3["out"], l3.at("out", ta.n))
                    after_wait(pool)
                    ge(pool, l3_put[ta.b], 16 * R * ta.i)
                    indices(put_at[:, ta.b], skip_or_dst, ta.g * R, R, l3_ix_put, ta.n)
                    for r in range(R):
                        POOL.indirect_dma_start(
                            a["out"], bass.IndirectOffsetOnAxis(ap=put_at[:, ta.b, r:r + 1], axis=0),
                            oA[:, ta.b, r, :], None, bounds_check=N - 1,
                            oob_is_err=False).then_inc(l3_put[ta.b], 16)
                if ba is not None:
                    pool.wait_ge(l3["var"], 3 * ba.n)
                    ge(pool, l3["out"], l3.at("out", ba.n - 1))
                    inverse_root(r2[:], vin2[:]).then_inc(l3["pw"], 1)
            passes(POOL.Fori, "E", 3, l3_step)

        @block.tensor
        def _(pe):
            def transposes(out, src):
                for r in range(R):
                    mm = pe.transpose(out[:, r * P:(r + 1) * P], src(r), ident[:])
                return mm

            def rows_times(out, lhs, rhs):
                for r in range(R):
                    mm = pe.matmul(out[:, r * D:(r + 1) * D], lhs[:, r, :], rhs, start=True, stop=True)
                return mm

            def gram(bank, lhs, rhs):
                for r in range(R):
                    mm = pe.matmul(bank[:, 0:D + 1], lhs(r), rhs(r), start=False, stop=True, skip_group_check=True)
                return mm

            pe.wait_ge(pool_const, POOL_CONST)
            pe.wait_ge(const_loaded, CONST)
            pe.transpose(pm1[:, 0:D], W1[:], ident[:])
            pe.transpose(pm1[:, D:2 * D], W2[:], ident[:]).then_inc(setup_pe, 1)
            pe.matmul(pG[:, 0:D + 1], ident[:], gm[:, 0, :], start=True, stop=True)
            pe.wait_ge(setup_dve, ROWS_READY)
            for c in range(5):
                mm = pe.transpose(pm2[:, ET * c:ET * (c + 1)], rows_f[:, c, :], ident[0:ET, 0:ET])
            mm.then_inc(setup_pe, 1)

            def step(i, k, fr, mi, ba, ta, od, work=None):
                def mm3(c):
                    if c == 0:
                        pe.wait_ge(n2_made, ba.n)
                    ge(pe, gelu_made, 4 * ba.g + c - 1)
                    pe.matmul(pm3[c % 2][:], Wf1[:, c * P:(c + 1) * P], f(w["n2"][:]), start=True,
                              stop=True).then_inc(mm3_done, 1)

                if mi is not None:
                    if mi.kind == "N":
                        pe.wait_ge(h_made, mi.n)
                    else:
                        pe.wait_ge(he_made, mi.j + 1)
                    ge(pe, r_made, mi.n - 1)
                    if isinstance(mi.i, int) and mi.g == 0:
                        pe.wait_ge(setup_dve, SETUP_DVE)
                    pe.matmul(pm1[:], Wg1[:], f(w["h"][:]), start=True, stop=True).then_inc(mm1_done, 1)
                if ba is not None:
                    mm3(0)
                    mm3(1)
                if mi is not None:
                    pe.wait_ge(r_made, mi.n)
                    ge(pe, x1_made, mi.n - 1)
                    rows_times(pm2, w["r"], Wg2[:]).then_inc(mm2_done, 1)
                if ba is not None:
                    mm3(2)
                    mm3(3)
                if fr is not None and fr.kind == "E":
                    pe.wait_ge(xhs_made, fr.j + 1)
                    pe.wait_ge(h_made, NG)
                    ge(pe, hraw_made, fr.j)
                    transposes(pT1, lambda r: w["xhs"][:, r, :]).then_inc(ts_done, 1)
                    pe.wait_ge(attr_got[fr.b], 16 * R * (fr.i - NG // 2 + 1))
                    pe.wait_ge(n2_made, fr.n - 2)
                    transposes(pT2, lambda r: at[:, fr.b, r, :]).then_inc(ta_done, 1)
                if fr is not None:
                    pe.wait_ge(xh1_made, fr.n)
                    if fr.kind == "N":
                        ge(pe, h_made, fr.n - 1)
                    else:
                        pe.wait_ge(ms_made, fr.j + 1)
                    transposes(pT1, lambda r: w["xh1"][:, r, :]).then_inc(t1_done, 1)
                if ba is not None:
                    pe.wait_ge(gelu_made, 4 * ba.n)
                    ge(pe, u_made, ba.n - 1)
                    for r in range(R):
                        for c in range(4):
                            mm = pe.matmul(pm4[:, r * D:(r + 1) * D], gT[:, c, r * P:(r + 1) * P], Wf2[:, c, :],
                                           start=(c == 0), stop=(c == 3))
                    mm.then_inc(mm4_done, 1)
                if mi is not None:
                    pe.wait_ge(xh2_made, mi.n)
                    ge(pe, n2_made, mi.n - 1)
                    if fr is not None and fr.kind == "E":
                        pe.wait_ge(ma_made, fr.j + 1)
                    transposes(pT2, lambda r: w["xh2"][:, r, :]).then_inc(t2_done, 1)
            run_pipeline(nc.tensor.Fori, step)

            def l1_step(q, before):
                if q is not None:
                    pe.wait_ge(l1_got[q.b], 16 * R * (q.i + 1))
                    pe.wait_ge(l1["same"], l1.at("same", q.n))
                    ge(pe, l1["rows"], l1.at("rows", q.n - 1))
                    for r in range(R):
                        for c in range(R):
                            mm = pe.matmul(pm1[:, r * D:(r + 1) * D], gT[:, c, r * P:(r + 1) * P], gr[:, q.b, c, :],
                                           start=(c == 0), stop=(c == R - 1))
                    mm.then_inc(l1["sum"], 1)
            edge_groups(nc.tensor.Fori, l1_step)

            def nb_step(coming, p, before):
                if before is not None:
                    pe.wait_ge(nb["m"], nb.at("m", before.n))
                    gram(pG, lambda r: oA[:, before.b, r, :], lambda r: gms[before.b][:, r, :]).then_inc(nb["gram"], 1)
            batch_pass(nc.tensor.Fori, nb_step)

            pe.wait_ge(u_made, PIPE)
            pe.matmul(pm4[:, 0:D + 1], ident[:], zero_row[:, 0:D + 1], start=True, stop=True)

            def l2_step(q, before):
                if q is not None:
                    pe.wait_ge(l2_got[q.b], 16 * R * (q.i + 1))
                    ge(pe, l2["scan"], l2.at("scan", q.n - 1))
                    transposes(pT1, lambda r: gr[:, q.b, r, :]).then_inc(l2["t"], 1)
                    pe.wait_ge(l2["scan"], l2.at("scan", q.n))
                    ge(pe, l2["g"], l2.at("g", q.n - 1))
                    agg = w["f1"] if q.b else w["f0"]
                    transposes(pT2, lambda r: agg[:, r, :]).then_inc(l2["tb"], 1)
                if before is not None:
                    pe.wait_ge(l2["g"], l2.at("g", before.n))
                    ge(pe, l2["gt"], l2.at("gt", before.n - 1))
                    transposes(pm1, lambda r: ub[:, before.b, r, :]).then_inc(l2["tg"], 1)
                    pe.wait_ge(l2["gm"], l2.at("gm", before.n))
                    gram(pm4, lambda r: ub[:, before.b, r, :], lambda r: gm[:, r, :]).then_inc(l2["gram"], 1)
                    pe.wait_ge(l2["gt"], l2.at("gt", before.n))
                    ge(pe, l2["h"], l2.at("h", before.n - 1))
                    pe.matmul(pm2[:], W1T[:], f(w["n2"][:]), start=True, stop=True).then_inc(l2["mm"], 1)
            edge_groups(nc.tensor.Fori, l2_step)

            pe.wait_ge(bns["dve"], BN_COV)
            pe.matmul(pm1[:, 0:D], cov[:, 0:D], W1T[:], start=True, stop=True)
            pe.matmul(pm1[:, D:D + 1], W1T[:], cov[:, D:D + 1], start=True, stop=True).then_inc(bns["pe"], 1)
            pe.wait_ge(bns["dve"], BN_QUAD)
            pe.matmul(pm3[0][:, 0:1], covE[:, 0:D], ones[:, 0:1], start=True, stop=True).then_inc(bns["pe"], 1)

            def biased(out, lhs, rhs, bias):
                pe.matmul(out[:], ones[0:1, :], bcast(bias)[0:1], start=True, stop=True)
                for r in range(R):
                    mm = pe.matmul(out[:, r * D:(r + 1) * D], lhs[:, r, :], rhs, start=False, stop=True,
                                   skip_group_check=True)
                return mm

            def q2_step(q, mi, ba):
                if q is not None:
                    pe.wait_ge(q2["r"], q2.at("r", q.n))
                    ge(pe, q2["rt"], q2.at("rt", q.n - 1))
                    pe.wait_ge(l2["h"], l2.at("h", EG))
                    biased(pm2, w["r"], W2T[:], b2r).then_inc(q2["mm"], 1)
            passes(nc.tensor.Fori, "E", 2, q2_step)

            def n2_step(p, mi, ba, ta, la):
                if p is not None:
                    pe.wait_ge(n2_loaded[p.b], 16 * (p.i + 1))
                    ge(pe, n2["c"], n2.at("c", p.n - 1))
                    transposes(pT1, lambda r: xin[:, p.b, r, :]).then_inc(n2["ta"], 1)
                if mi is not None:
                    pe.wait_ge(n2["r"], n2.at("r", mi.n))
                    ge(pe, n2["rt"], n2.at("rt", mi.n - 1))
                    biased(pm2, w["r"], W2T[:], b2r).then_inc(n2["mm2"], 1)
                if ba is not None:
                    pe.wait_ge(n2["xc"], n2.at("xc", ba.n))
                    ge(pe, n2["ct"], n2.at("ct", ba.n - 1))
                    transposes(pT2, lambda r: oA[:, ba.b, r, :]).then_inc(n2["tc"], 1)
                if p is not None:
                    pe.wait_ge(n2["c"], n2.at("c", p.n))
                    ge(pe, n2["r"], n2.at("r", p.n - 1))
                    pe.matmul(pm1[:], W1T[:], f(w["h"][:]), start=True, stop=True).then_inc(n2["mm1"], 1)
                if ba is not None:
                    pe.wait_ge(n2["ct"], n2.at("ct", ba.n))
                    ge(pe, n2["z"], n2.at("z", ba.n - 1))
                    rows_times(pm4, w["n2"], Ws[:]).then_inc(n2["mm3"], 1)
            node_passes(nc.tensor.Fori, n2_step)

            def l3_step(q, mi, ba, ta):
                if q is not None:
                    pe.wait_ge(l3_got[q.b], 16 * R * (q.i + 1))
                    ge(pe, l3["xd"], l3.at("xd", q.n - 1))
                    transposes(pT1, lambda r: gr[:, q.b, r, :]).then_inc(l3["ts"], 1)
                    pe.wait_ge(l3["cp"], l3.at("cp", q.n))
                    pe.wait_ge(l3["xs"], l3.at("xs", q.n))
                    transposes(pT1, lambda r: w["xh1"][:, r, :]).then_inc(l3["td"], 1)
                if ba is not None:
                    pe.wait_ge(l3["den"], l3.at("den", ba.n))
                    ge(pe, l3["z"], l3.at("z", ba.n - 1))
                    transposes(pG, lambda r: nums[ba.b][:, r, :])
                    for r in range(R):
                        mm = pe.matmul(pT2[:, r:r + 1], dens[ba.b][0:1, r, :], ones[0:1, 0:1], start=True, stop=True)
                    mm.then_inc(l3["tn"], 1)
                if q is not None:
                    pe.wait_ge(l3["xd"], l3.at("xd", q.n))
                    ge(pe, l3["q"], l3.at("q", q.n - 1))
                    pe.matmul(pm1[:], Wq[:], f(w["n2"][:]), start=True, stop=True).then_inc(l3["mq"], 1)
                    ge(pe, l3["qk"], l3.at("qk", q.n - 1))
                    pe.matmul(pm2[:], Wk[:], f(w["h"][:]), start=True, stop=True).then_inc(l3["mk"], 1)
                    ge(pe, l3["base"], l3.at("base", q.n - 1))
                    biased(pm4, w["n2"], Ws[:], bsr).then_inc(l3["mm"], 1)
                    pe.wait_ge(l3["qk"], l3.at("qk", q.n))
                    ge(pe, l3["l"], l3.at("l", q.n - 1))
                    pe.matmul(pm3[1][:], ones[:], f(w["msg"][:]), start=True, stop=True).then_inc(l3["ml"], 1)
                    ge(pe, l3["num"], l3.at("num", q.n - 1))
                    pe.matmul(pm3[0][:], Wv[:], f(w["h"][:]), start=True, stop=True).then_inc(l3["mv"], 1)
            passes(nc.tensor.Fori, "E", 3, l3_step)

        @block.scalar
        def _(act):
            A = nc.scalar
            act.wait_ge(const_loaded, CONST)
            act.wait_ge(setup_dve, SETUP_DVE)
            act.wait_ge(pool_const, POOL_CONST)

            def scale_rows(out, src, scale, bias):
                for r in range(R):
                    last = A.activation(out(r), src(r), ACT.Identity, bias=bias(r), scale=scale(r))
                return last

            def step(i, k, fr, mi, ba, ta, od, work=None):
                def gelu(c):
                    if c == 0:
                        ge(act, mm4_done, ba.n - 1)
                    act.wait_ge(mm3_done, 4 * ba.g + c + 1)
                    A.activation(gT[:, c, :], pm3[c % 2][:], ACT.Gelu, bias=bf1c[:, c:c + 1]).then_inc(gelu_made, 1)

                if mi is not None:
                    act.wait_ge(mm1_done, mi.n)
                    ge(act, mm2_done, mi.n - 1)
                    A.activation(f(w["r"][:]), pm1[:], ACT.Relu, bias=col["bg1"]).then_inc(r_made, 1)
                if ba is not None:
                    gelu(0)
                    gelu(1)
                if ta is not None:
                    act.wait_ge(nma_made, ta.n)
                    if ta.kind == "N":
                        ge(act, xA_stored[ta.b], 16 * ta.i)
                        out = lambda r: oA[:, ta.b, r, :]
                    else:
                        out = lambda r: tile(X, ta.j, r)
                    scale_rows(out, lambda r: ub[:, ta.b, r, :], lambda r: r3[:, ta.b, r:r + 1],
                               lambda r: nma[:, r:r + 1]).then_inc(xA_made, 1)
                if ba is not None:
                    gelu(2)
                    gelu(3)
                if fr is not None and fr.kind == "E":
                    act.wait_ge(ts_done, fr.j + 1)
                    ge(act, ma_made, fr.j)
                    A.activation(f(w["ms"][:]), pT1[:], ACT.Identity, bias=col["b1"], scale=col["g1"]).then_inc(ms_made, 1)
                if fr is not None:
                    act.wait_ge(t1_done, fr.n)
                    if fr.kind == "N":
                        ge(act, mm1_done, fr.n - 1)
                        A.activation(f(w["h"][:]), pT1[:], ACT.Identity, bias=b1s, scale=g1s).then_inc(h_made, 1)
                    else:
                        ge(act, he_made, fr.j)
                        A.activation(f(w["hraw"][:]), pT1[:], ACT.Identity, bias=b1s, scale=g1s).then_inc(hraw_made, 1)
                        act.wait_ge(ma_made, fr.j + 1)
                        ge(act, agg_made, fr.j)
                        A.activation(f(w["msg"][:]), f(w["ma"][:]), ACT.Relu).then_inc(msg_made, 1)
                if ta is not None:
                    act.wait_ge(nmb_made, 2 * ta.n)
                    if ta.kind == "N":
                        ge(act, y_stored[ta.b], 16 * ta.i)
                    else:
                        act.wait_ge(y_stored[ta.b], 16 * PAIRS_N)
                        ge(act, y_put[ta.b], 16 * R * (ta.i - NG // 2))
                    scale_rows(lambda r: oB[:, ta.b, r, :], lambda r: ub[:, ta.b, r, :],
                               lambda r: rb[:, r:r + 1], lambda r: nmb[:, r:r + 1]).then_inc(y_made, 1)
                if mi is not None:
                    act.wait_ge(t2_done, mi.n)
                    ge(act, mm3_done, 4 * (mi.n - 1))
                    A.activation(f(w["n2"][:]), pT2[:], ACT.Identity, bias=col["b2"], scale=col["g2"]).then_inc(n2_made, 1)

            run_pipeline(A.Fori, step)

            def l1_step(q, before):
                if q is not None:
                    act.wait_ge(l1["sum"], l1.at("sum", q.n))
                    ge(act, l1_added[q.b], 16 * R * q.i)
                    for b in range(2):
                        act.wait_ge(xA_stored[b], 16 * PAIRS_N)
                    A.copy(f(oA[:, q.b]), pm1[:]).then_inc(l1["rows"], 1)
            edge_groups(A.Fori, l1_step)

            def nb_step(coming, p, before):
                if before is not None:
                    act.wait_ge(nb["x"], nb.at("x", before.n))
                    ge(act, nb["gram"], nb.at("gram", before.n - 2))
                    A.copy(gms[before.b][:, :, D:D + 1].rearrange("p r o -> p (r o)"), open_rows[:, span(before.g, 1), :].rearrange("p o r -> p (o r)"))
                    for r in range(R):
                        last = A.activation(gms[before.b][:, r, 0:D], oA[:, before.b, r, :], ACT.Identity,
                                            scale=open_rows[:, span(before.g, 1), r:r + 1].rearrange("p o r -> p (o r)"))
                    last.then_inc(nb["m"], 1)
            batch_pass(A.Fori, nb_step)

            def l2_step(q, before):
                if q is not None:
                    act.wait_ge(l2_own[q.b], 16 * R * (q.i + 1))
                    A.copy(X[:, span(q.g * R, R), :], at[:, q.b]).then_inc(l2["x"], 1)
                if before is not None:
                    act.wait_ge(nb["gram"], NG)
                    act.wait_ge(l2["g"], l2.at("g", before.n))
                    ge(act, l2["gram"], l2.at("gram", before.n - 1))
                    A.copy(gm[:, :, D:D + 1].rearrange("p r o -> p (r o)"), is_last[:, span(before.g * R, R)])
                    for r in range(R):
                        last = A.activation(gm[:, r, 0:D], ub[:, before.b, r, :], ACT.Identity,
                                            scale=is_last[:, span(before.g * R + r, 1)])
                    last.then_inc(l2["gm"], 1)
                    act.wait_ge(l2["tg"], l2.at("tg", before.n))
                    ge(act, l2["mm"], l2.at("mm", before.n - 1))
                    A.copy(f(w["n2"][:]), pm1[:]).then_inc(l2["gt"], 1)
                    act.wait_ge(l2["mm"], l2.at("mm", before.n))
                    A.copy(HT[:, span(before.g * G, G)], pm2[:]).then_inc(l2["h"], 1)
            edge_groups(A.Fori, l2_step)

            act.wait_ge(bns["ready"], BN_DONE)

            def q2_step(q, mi, ba):
                if mi is not None:
                    act.wait_ge(q2["mm"], q2.at("mm", mi.n))
                    ge(act, q2["y"], q2.at("y", mi.n - 1))
                    A.activation(f(w["ms"][:]), pm2[:], ACT.Relu).then_inc(q2["rt"], 1)
                if q is not None:
                    ge(act, q2["mm"], q2.at("mm", q.n - 1))
                    act.wait_ge(l2["h"], l2.at("h", EG))
                    A.activation(f(w["r"][:]), HT[:, span(q.g * G, G)], ACT.Relu, bias=bn_b, scale=bn_a).then_inc(q2["r"], 1)
            passes(A.Fori, "E", 2, q2_step)

            def n2_step(p, mi, ba, ta, la):
                if p is not None:
                    act.wait_ge(n2["ta"], n2.at("ta", p.n))
                    ge(act, n2["mm1"], n2.at("mm1", p.n - 1))
                    A.activation(f(w["h"][:]), pT1[:], ACT.Identity, scale=one_e2).then_inc(n2["c"], 1)
                if mi is not None:
                    act.wait_ge(n2["mm2"], n2.at("mm2", mi.n))
                    ge(act, n2["y"], n2.at("y", mi.n - 1))
                    A.activation(f(w["ms"][:]), pm2[:], ACT.Relu).then_inc(n2["rt"], 1)
                if ba is not None:
                    act.wait_ge(n2["tc"], n2.at("tc", ba.n))
                    ge(act, n2["mm3"], n2.at("mm3", ba.n - 1))
                    A.copy(f(w["n2"][:]), pT2[:]).then_inc(n2["ct"], 1)
                if p is not None:
                    act.wait_ge(n2["mm1"], n2.at("mm1", p.n))
                    ge(act, n2["mm2"], n2.at("mm2", p.n - 1))
                    A.activation(f(w["r"][:]), pm1[:], ACT.Relu, bias=bn_b, scale=bn_a).then_inc(n2["r"], 1)
                if la is not None:
                    act.wait_ge(n2["nm"], n2.at("nm", la.n))
                    ge(act, n2_ost[la.b], 16 * la.i)
                    scale_rows(lambda r: s2b[:, la.b, r, :], lambda r: ub[:, la.b, r, :],
                               lambda r: r3[:, la.b, r:r + 1], lambda r: nma[:, r:r + 1]).then_inc(n2["o"], 1)
            node_passes(A.Fori, n2_step)

            act.wait_ge(own_kept, 16 * EG)

            def l3_step(q, mi, ba, ta):
                if q is not None:
                    ge(act, l3["td"], l3.at("td", q.n - 1))
                    A.copy(w["xh1"][:], X[:, span(q.g * R, R), :]).then_inc(l3["cp"], 1)
                    act.wait_ge(l3["ts"], l3.at("ts", q.n))
                    ge(act, l3["mv"], l3.at("mv", q.n - 1))
                    A.copy(f(w["h"][:]), pT1[:]).then_inc(l3["xs"], 1)
                    act.wait_ge(l3["td"], l3.at("td", q.n))
                    ge(act, l3["mm"], l3.at("mm", q.n - 1))
                    A.copy(f(w["n2"][:]), pT1[:]).then_inc(l3["xd"], 1)
                if mi is not None:
                    ge(act, l3["e1"], l3.at("e1", mi.n - 1))
                    A.activation(f(w["hraw"][:]), keep[:, span(mi.g * G, G)], ACT.Identity, bias=mbig[:], scale=BIG).then_inc(l3["pen"], 1)
                    act.wait_ge(l3["ml"], l3.at("ml", mi.n))
                    ge(act, l3["lm"], l3.at("lm", mi.n - 1))
                    A.activation(f(w["ms"][:]), pm3[1][:], ACT.Identity, scale=SM_SCALE).then_inc(l3["l"], 1)
                if q is not None:
                    act.wait_ge(l3["mq"], l3.at("mq", q.n))
                    ge(act, l3["qk"], l3.at("qk", q.n - 1))
                    A.activation(f(w["r"][:]), pm1[:], ACT.Identity, bias=col["bq"]).then_inc(l3["q"], 1)
                if mi is not None:
                    act.wait_ge(l3["e2"], l3.at("e2", mi.n))
                    ge(act, l3["den"], l3.at("den", mi.n - 1))
                    A.activation(f(w["xb"][:]), f(w["x1"][:]), ACT.Exp).then_inc(l3["c"], 1)
                    act.wait_ge(l3["lm"], l3.at("lm", mi.n))
                    A.activation(f(w["xc"][:]), f(w["xh2"][:]), ACT.Exp).then_inc(l3["p"], 1)
            passes(A.Fori, "E", 3, l3_step)

        @block.vector
        def _(dve):
            V = nc.vector

            def stats(src, k, s, n):
                for r in range(R):
                    last = V.bn_stats(stt[:, k, r, :], src(r))
                last.then_inc(s, 1)
                dve.wait_ge(s, 3 * n - 2)
                after_wait(dve)
                for r in range(R):
                    last = V.bn_aggr(mv[:, k, r, :], stt[:, k, r, :])
                last.then_inc(s, 1)
                dve.wait_ge(s, 3 * n - 1)

            def normalise(out, src, k, scale):
                for r in range(R):
                    last = V.tensor_scalar(out(r), src(r), mv[:, k, r, 0:1], scale[:, r:r + 1], ALU.subtract, ALU.mult)
                return last

            def variance(out, k):
                return V.tensor_scalar(out, mv[:, k, :, 1], LN_EPS, None, ALU.add)

            dve.wait_ge(const_loaded, CONST)
            V.tensor_scalar(one_eg, eps3[:, 0:1], 1.0, None, ALU.add).then_inc(setup_dve, 1)
            V.tensor_scalar(two_e1, eps3[:, 1:2], 2.0, None, ALU.add).then_inc(setup_dve, 1)
            V.tensor_scalar(one_e2, eps3[:, 2:3], 1.0, None, ALU.add).then_inc(setup_dve, 1)
            V.memset(zero_row[:], 0.0).then_inc(setup_dve, 1)
            dve.wait_ge(pool_const, POOL_CONST)
            V.tensor_copy(spare[:], spare_i[:]).then_inc(setup_dve, 1)
            V.memset(mbig[:], -BIG).then_inc(setup_dve, 1)
            dve.wait_ge(setup_dve, 6)
            V.tensor_tensor(g1s, col["g1"], one_eg, ALU.mult).then_inc(setup_dve, 1)
            V.tensor_tensor(b1s, col["b1"], one_eg, ALU.mult).then_inc(setup_dve, 1)
            dve.wait_ge(tables_written, 16 * 14)
            V.tensor_copy(rows_f[:, 5, :], rows_i[:, 0, :]).then_inc(setup_dve, 1)
            V.tensor_copy(rows_f[:, 6, :], rows_i[:, 1, :]).then_inc(setup_dve, 1)
            V.tensor_copy(rows_f[:, 2, :], rows_i[:, 2, :]).then_inc(setup_dve, 1)
            V.tensor_copy(rows_f[:, 7, :], rows_i[:, 3, :]).then_inc(setup_dve, 1)
            dve.wait_ge(setup_dve, 12)
            V.tensor_tensor(rows_f[:, 4, :], rows_f[:, 5, :], rows_f[:, 6, :], ALU.is_equal).then_inc(setup_dve, 1)
            dve.wait_ge(setup_dve, 13)
            V.scalar_tensor_tensor(out=rows_f[:, 0, :], in0=rows_f[:, 4, :], scalar=float(FAR), in1=rows_f[:, 5, :],
                                   op0=ALU.mult, op1=ALU.add).then_inc(setup_dve, 1)
            V.tensor_scalar(rows_f[:, 1, :], rows_f[:, 5, :], float(N - 1), None, ALU.min).then_inc(setup_dve, 1)
            V.tensor_scalar(rows_f[:, 3, :], rows_f[:, 7, :], float(E - 1), None, ALU.min).then_inc(setup_dve, 1)
            dve.wait_ge(setup_pe, 1)
            V.tensor_copy(W1T[:], pm1[:, 0:D]).then_inc(setup_dve, 1)
            V.tensor_copy(W2T[:], pm1[:, D:2 * D]).then_inc(setup_dve, 1)
            dve.wait_ge(setup_pe, 2)
            for t, c in ((skip_or_dst, 0), (dst_i, 1), (perm_i, 3)):
                V.tensor_copy(t[:], pm2[:, ET * c:ET * (c + 1)]).then_inc(setup_dve, 1)
            V.tensor_scalar(is_last[:], pm2[:, 4 * ET:5 * ET], -1.0, 1.0, ALU.mult, ALU.add).then_inc(setup_dve, 1)
            V.tensor_copy(src_f[:], pm2[:, 2 * ET:3 * ET]).then_inc(setup_dve, 1)
            V.tensor_scalar(src_i[:], pm2[:, 2 * ET:3 * ET], float(N - 1), None, ALU.min).then_inc(setup_dve, 1)
            dve.wait_ge(setup_dve, SETUP_DVE)
            dve.wait_ge(pool_const, POOL_CONST)

            def step(i, k, fr, mi, ba, ta, od, work=None):
                if fr is not None:
                    if fr.kind == "N":
                        dve.wait_ge(x_loaded[fr.b], 16 * (fr.i + 1))
                        x, xall = (lambda r: xin[:, fr.b, r, :]), xin[:, fr.b]
                    else:
                        dve.wait_ge(pre_kept[0], 16 * EG)
                        dve.wait_ge(pre_kept[1], 16 * EG)
                        x, xall = (lambda r: tile(X, fr.j, r)), X[:, span(fr.j * R, R), :]
                        stats(lambda r: tile(H, fr.j, r), 3, var["s"], fr.j + 1)
                        variance(vinc[:, 4:8], 3).then_inc(var["s"], 1)
                    stats(x, 0, var["1"], fr.n)
                    variance(vinc[:, 0:4], 0).then_inc(var["1"], 1)
                if ta is not None:
                    dve.wait_ge(pow3, ta.n)
                    ge(dve, xA_made, ta.n - 1)
                    V.scalar_tensor_tensor(out=nma[:], in0=mv[:, 2, :, 0], scalar=-1.0, in1=r3[:, ta.b],
                                           op0=ALU.mult, op1=ALU.mult).then_inc(nma_made, 1)
                    ge(dve, y_made, ta.n - 1)
                    V.tensor_scalar(rb[:], r3[:, ta.b], two_e1, None, ALU.mult).then_inc(nmb_made, 1)
                    dve.wait_ge(nma_made, ta.n)
                    V.tensor_scalar(nmb[:], nma[:], two_e1, None, ALU.mult).then_inc(nmb_made, 1)
                if mi is not None:
                    dve.wait_ge(mm2_done, mi.n)
                    dve.wait_ge(xb_made, mi.n)
                    ge(dve, s_made, mi.n - 1)
                    V.tensor_tensor(f(w["x1"][:]), pm2[:], f(w["xb"][:]), ALU.add).then_inc(x1_made, 1)
                if fr is not None:
                    dve.wait_ge(powc, fr.n)
                    if fr.kind == "E":
                        ge(dve, ts_done, fr.j)
                        normalise(lambda r: w["xhs"][:, r, :], lambda r: tile(H, fr.j, r), 3, ro[:, 4:8]).then_inc(xhs_made, 1)
                    ge(dve, t1_done, fr.n - 1)
                    normalise(lambda r: w["xh1"][:, r, :], x, 0, ro[:, 0:4]).then_inc(xh1_made, 1)
                if mi is not None:
                    dve.wait_ge(x1_made, mi.n)
                    stats(lambda r: w["x1"][:, r, :], 1, var["2"], mi.n)
                    variance(vin2[:], 1).then_inc(var["2"], 1)
                    dve.wait_ge(xc_made, mi.n)
                    V.tensor_tensor(s2b[:, mi.b], w["xc"][:], w["x1"][:], ALU.add).then_inc(s_made, 1)
                if fr is not None:
                    ge(dve, x1_made, fr.n - 1)
                    V.tensor_tensor(w["xb"][:], xall, bcast(bg2r), ALU.add).then_inc(xb_made, 1)
                    ge(dve, s_made, fr.n - 1)
                    V.tensor_tensor(w["xc"][:], xall, bcast(bf2r), ALU.add).then_inc(xc_made, 1)
                if mi is not None:
                    dve.wait_ge(pow2, mi.n)
                    ge(dve, t2_done, mi.n - 1)
                    normalise(lambda r: w["xh2"][:, r, :], lambda r: w["x1"][:, r, :], 1, r2).then_inc(xh2_made, 1)
                if fr is not None and fr.kind == "E":
                    dve.wait_ge(ms_made, fr.j + 1)
                    dve.wait_ge(ta_done, fr.j + 1)
                    ge(dve, msg_made, fr.j)
                    V.tensor_tensor(f(w["ma"][:]), pT2[:], f(w["ms"][:]), ALU.add).then_inc(ma_made, 1)
                if fr is not None and fr.kind == "E":
                    dve.wait_ge(keep_made, KC)
                    dve.wait_ge(msg_made, fr.j + 1)
                    agg, before = (w["f1"], w["f0"]) if fr.b else (w["f0"], w["f1"])
                    if isinstance(fr.i, int) and fr.j == 0:
                        first = 0.0
                    else:
                        first = before[:, R - 1, D - 1:D]
                        dve.wait_ge(agg_made, fr.j)
                    V.tensor_tensor_scan(f(agg[:]), keep[:, span(fr.j * G, G)], f(w["msg"][:]), first,
                                         ALU.mult, ALU.add).then_inc(agg_made, 1)
                    dve.wait_ge(agg_made, fr.j + 1)
                    dve.wait_ge(hraw_made, fr.j + 1)
                    dve.wait_ge(mm1_done, fr.n - 1)
                    V.tensor_tensor(w["h"][:], w["hraw"][:], agg[:], ALU.add).then_inc(he_made, 1)
                if work == "pre":
                    c = 2 * (i - PRE_GOT) + k
                    dve.wait_ge(dst_row_loaded[k], 16 * (i - PRE_GOT + 1))
                    V.tensor_tensor(keep[:, span(c * KW, KW)], dst_row[k][:, 1:KW + 1], dst_row[k][:, 0:KW],
                                    ALU.is_equal).then_inc(keep_made, 1)
                if ba is not None:
                    dve.wait_ge(mm4_done, ba.n)
                    dve.wait_ge(s_made, ba.n)
                    V.tensor_tensor(f(ub[:, ba.b]), pm4[:], f(s2b[:, ba.b]), ALU.add).then_inc(u_made, 1)
                    dve.wait_ge(u_made, ba.n)
                    stats(lambda r: ub[:, ba.b, r, :], 2, var["3"], ba.n)
                    variance(vin3[:], 2).then_inc(var["3"], 1)

            run_pipeline(V.Fori, step)

            def l1_step(q, before):
                if q is not None:
                    dve.wait_ge(l1_keys[q.b], 16 * (q.i + 1))
                    ge(dve, l1["sum"], l1.at("sum", q.n - 1))
                    for r in range(R):
                        last = V.tensor_scalar(gT[:, r, :], keys[:, q.b], src_f[:, span(q.g * R + r, 1)], None, ALU.is_equal)
                    last.then_inc(l1["same"], 1)
                    dve.wait_ge(l1["same"], l1.at("same", q.n))
                    for r in range(R):
                        last = V.tensor_tensor_reduce(out=l1_junk[r], in0=gT[:, r, :], in1=later_mask[:, r, :], scale=1.0,
                                                      scalar=0.0, op0=ALU.mult, op1=ALU.add, accum_out=sm[:, 0, r:r + 1])
                    last.then_inc(l1["count"], 1)
                    own = src_f[:, span(q.g * R, R)]
                    V.tensor_scalar(sm[:, 1, :], own, float(N), None, ALU.is_ge).then_inc(l1["far"], 1)
                    dve.wait_ge(l1["far"], l1.at("far", q.n))
                    V.scalar_tensor_tensor(out=sm[:, 2, :], in0=sm[:, 0, :], scalar=0.0, in1=sm[:, 1, :],
                                           op0=ALU.is_gt, op1=ALU.max).then_inc(l1["dup"], 1)
                    V.tensor_tensor(sm[:, 3, :], spare[:], own, ALU.subtract).then_inc(l1["away"], 1)
                    dve.wait_ge(l1["away"], l1.at("away", q.n))
                    V.tensor_tensor(sm[:, 4, :], sm[:, 3, :], sm[:, 2, :], ALU.mult).then_inc(l1["mul"], 1)
                    dve.wait_ge(l1["mul"], l1.at("mul", q.n))
                    ge(dve, l1_added[q.b], 16 * R * q.i)
                    V.tensor_tensor(sums_at[:, q.b, 0:R], sm[:, 4, :], own, ALU.add).then_inc(l1["idx"], 1)
            dve.wait_ge(pool_const, POOL_CONST + 2)
            for b in range(2):
                dve.wait_ge(y_put[b], 16 * R * ((EG + 1 - b) // 2))
            edge_groups(V.Fori, l1_step)

            dve.wait_ge(open_loaded, 16 * NG)
            V.tensor_scalar(open_rows[:], open_i[:], float(N), None, ALU.is_lt).then_inc(setup_dve, 1)
            dve.wait_ge(setup_dve, SETUP_DVE + 1)
            V.tensor_scalar(open_rows[:, NG - 1, :], open_rows[:, NG - 1, :], fresh[:], None, ALU.mult).then_inc(setup_dve, 1)
            dve.wait_ge(l1["rows"], l1.at("rows", EG))
            for b in range(2):
                dve.wait_ge(l1_added[b], 16 * R * ((EG + 1 - b) // 2))

            def nb_step(coming, p, before):
                if before is not None:
                    dve.wait_ge(nb["pw"], nb.at("pw", before.n))
                    ge(dve, nb_stored[before.b], 16 * before.i)
                    ge(dve, nb["gram"], nb.at("gram", before.n - 2))
                    normalise(lambda r: oA[:, before.b, r, :], lambda r: before.rows[:, r, :], before.b, r3[:, before.b]).then_inc(nb["x"], 1)
                if p is not None:
                    dve.wait_ge(nb_loaded[p.b], 16 * (p.i + 1))
                    ge(dve, nb["x"], nb.at("x", p.n - 2))
                    stats(lambda r: p.rows[:, r, :], p.b, nb["var"], p.n)
                    variance(vin_nb[p.b][:], p.b).then_inc(nb["var"], 1)
            batch_pass(V.Fori, nb_step)

            def scanned(q, s, n):
                agg, before = (w["f1"], w["f0"]) if q.b else (w["f0"], w["f1"])
                if isinstance(q.i, int) and q.g == 0:
                    first = 0.0
                else:
                    first = before[:, R - 1, D - 1:D]
                    dve.wait_ge(s["scan"], s.at("scan", n - 1))
                V.tensor_tensor_scan(f(agg[:]), keep[:, span(q.g * G, G)], pT1[:], first,
                                     ALU.mult, ALU.add).then_inc(s["scan"], 1)

            def l2_step(q, before):
                if q is not None:
                    dve.wait_ge(l2["t"], l2.at("t", q.n))
                    ge(dve, l2["tb"], l2.at("tb", q.n - 2))
                    scanned(q, l2, q.n)
                    dve.wait_ge(l2["tb"], l2.at("tb", q.n))
                    dve.wait_ge(l2_own[q.b], 16 * R * (q.i + 1))
                    ge(dve, l2["gram"], l2.at("gram", q.n - 2))
                    ge(dve, l2["gm"], l2.at("gm", q.n - 2))
                    V.scalar_tensor_tensor(out=ub[:, q.b], in0=at[:, q.b], scalar=one_e2,
                                           in1=pT2[:].rearrange("p (r d) -> p r d", r=R), op0=ALU.mult,
                                           op1=ALU.add).then_inc(l2["g"], 1)
            edge_groups(V.Fori, l2_step)

            for b in range(2):
                dve.wait_ge(new_kept[b], 32 * MAP_PAIRS)
            dve.wait_ge(l2["ix"], l2.at("ix", 2 * EG))
            V.tensor_scalar(newd_edge[:], newd_i[:], float(-N), 0.0, ALU.add, ALU.max).then_inc(setup_dve, 1)

            dve.wait_ge(l2["gram"], l2.at("gram", EG))
            dve.wait_ge(nb["gram"], NG)
            B, dn = bns["dve"], [0]

            def chain(ins):
                ins.then_inc(B, 1)
                dn[0] += 1
                dve.wait_ge(B, dn[0])
            chain(V.tensor_copy(covE[:], pm4[:, 0:D + 1]))
            chain(V.tensor_scalar(cov[:], pG[:, 0:D + 1], one_e2, None, ALU.mult))
            chain(V.scalar_tensor_tensor(out=cov[:, 0:D], in0=cov[:, 0:D], scalar=one_e2, in1=covE[:, 0:D],
                                         op0=ALU.mult, op1=ALU.add))
            chain(V.tensor_tensor(cov[:, D:D + 1], cov[:, D:D + 1], covE[:, D:D + 1], ALU.add))
            chain(V.tensor_scalar(cov[:], cov[:], 1.0 / N, None, ALU.mult))
            assert dn[0] == BN_COV
            dve.wait_ge(bns["pe"], 1)
            chain(V.tensor_tensor(covE[:, 0:D], pm1[:, 0:D], W1T[:], ALU.mult))
            chain(V.tensor_copy(bn[:, 0:1], pm1[:, D:D + 1]))
            assert dn[0] == BN_QUAD
            dve.wait_ge(bns["pe"], 2)
            chain(V.tensor_tensor(bn[:, 1:2], bn[:, 0:1], bn[:, 0:1], ALU.mult))
            chain(V.tensor_copy(bn[:, 2:3], pm3[0][:, 0:1]))
            chain(V.tensor_tensor(bn[:, 3:4], bn[:, 2:3], bn[:, 1:2], ALU.subtract))
            chain(V.tensor_scalar(bn[:, 4:5], bn[:, 3:4], 0.0, BN_EPS, ALU.max, ALU.add))
            assert dn[0] == BN_VAR
            dve.wait_ge(bns["pw"], 1)
            chain(V.tensor_tensor(bn_a, bn[:, 5:6], col["gamma"], ALU.mult))
            chain(V.tensor_tensor(bn[:, 6:7], bn[:, 0:1], col["L2b1"], ALU.add))
            chain(V.tensor_tensor(bn[:, 7:8], col["L2b1"], bn[:, 6:7], ALU.subtract))
            chain(V.tensor_tensor(bn[:, 8:9], bn[:, 7:8], bn_a, ALU.mult))
            V.tensor_tensor(bn_b, bn[:, 8:9], col["beta"], ALU.add).then_inc(bns["ready"], BN_DONE)

            dve.wait_ge(l2["x"], EG)

            def q2_step(q, mi, ba):
                if ba is not None:
                    dve.wait_ge(q2["pw"], q2.at("pw", ba.n))
                    normalise(lambda r: tile(X, ba.g, r), lambda r: ub[:, ba.b, r, :], 1, r2).then_inc(q2["x"], 1)
                if mi is not None:
                    dve.wait_ge(q2["rt"], q2.at("rt", mi.n))
                    V.scalar_tensor_tensor(out=ub[:, mi.b], in0=X[:, span(mi.g * R, R), :], scalar=2.0, in1=w["ms"][:],
                                           op0=ALU.mult, op1=ALU.add).then_inc(q2["y"], 1)
                    dve.wait_ge(q2["y"], q2.at("y", mi.n))
                    ge(dve, q2["x"], q2.at("x", mi.n - 1))
                    stats(lambda r: ub[:, mi.b, r, :], 1, q2["var"], mi.n)
                    variance(vin2[:], 1).then_inc(q2["var"], 1)
            passes(V.Fori, "E", 2, q2_step)

            def n2_step(p, mi, ba, ta, la):
                if la is not None:
                    dve.wait_ge(n2["pw2"], n2.at("pw2", la.n))
                    ge(dve, n2["o"], n2.at("o", la.n - 1))
                    V.scalar_tensor_tensor(out=nma[:], in0=mv[:, 2, :, 0], scalar=-1.0, in1=r3[:, la.b],
                                           op0=ALU.mult, op1=ALU.mult).then_inc(n2["nm"], 1)
                if ba is not None:
                    dve.wait_ge(n2["pw"], n2.at("pw", ba.n))
                    ge(dve, n2_cst[ba.b], 16 * ba.i)
                    ge(dve, n2["tc"], n2.at("tc", ba.n - 2))
                    ge(dve, n2["xcb"], n2.at("xcb", ba.n - 2))
                    normalise(lambda r: oA[:, ba.b, r, :], lambda r: w["xh1"][:, r, :], 1, r2).then_inc(n2["xc"], 1)
                if ta is not None:
                    dve.wait_ge(n2["mm3"], n2.at("mm3", ta.n))
                    dve.wait_ge(n2["xcb"], n2.at("xcb", ta.n))
                    ge(dve, n2["o"], n2.at("o", ta.n - 2))
                    V.tensor_tensor(f(ub[:, ta.b]), pm4[:], f(w["xb"][:]), ALU.add).then_inc(n2["z"], 1)
                    dve.wait_ge(n2["z"], n2.at("z", ta.n))
                    ge(dve, n2["nm"], n2.at("nm", ta.n - 1))
                    stats(lambda r: ub[:, ta.b, r, :], 2, n2["var2"], ta.n)
                    variance(vin3[:], 2).then_inc(n2["var2"], 1)
                if mi is not None:
                    dve.wait_ge(n2["rt"], n2.at("rt", mi.n))
                    dve.wait_ge(n2["x2"], n2.at("x2", mi.n))
                    ge(dve, n2["xc"], n2.at("xc", mi.n - 1))
                    V.tensor_tensor(w["xh1"][:], at[:, mi.b], w["ms"][:], ALU.add).then_inc(n2["y"], 1)
                    dve.wait_ge(n2["y"], n2.at("y", mi.n))
                    stats(lambda r: w["xh1"][:, r, :], 1, n2["var"], mi.n)
                    variance(vin2[:], 1).then_inc(n2["var"], 1)
            node_passes(V.Fori, n2_step)

            for b in range(2):
                dve.wait_ge(n2_cst[b], 16 * PAIRS_N)
                dve.wait_ge(n2_ost[b], 16 * PAIRS_N)
            dve.wait_ge(own_kept, 16 * EG)

            def l3_step(q, mi, ba, ta):
                if ta is not None:
                    dve.wait_ge(l3["pw"], l3.at("pw", ta.n))
                    ge(dve, l3_put[ta.b], 16 * R * ta.i)
                    normalise(lambda r: oA[:, ta.b, r, :], lambda r: ub[:, ta.b, r, :], 1, r2).then_inc(l3["out"], 1)
                if mi is not None:
                    n = mi.n
                    M, Mb = (w["f1"], w["f0"]) if mi.b else (w["f0"], w["f1"])
                    dve.wait_ge(l3["l"], l3.at("l", n))
                    first = isinstance(mi.i, int) and mi.g == 0
                    if not first:
                        dve.wait_ge(l3["m"], l3.at("m", n - 1))
                    V.tensor_tensor_scan(f(M[:]), f(w["hraw"][:]), f(w["ms"][:]), -BIG if first else Mb[:, R - 1, D - 1:D],
                                         ALU.add, ALU.max).then_inc(l3["m"], 1)
                    dve.wait_ge(l3["m"], l3.at("m", n))
                    ge(dve, l3["p"], l3.at("p", n - 1))
                    if first:
                        V.memset(w["xh2"][:, 0, 0:1], -BIG).then_inc(l3["carry"], 1)
                    else:
                        V.tensor_copy(w["xh2"][:, 0, 0:1], Mb[:, R - 1, D - 1:D]).then_inc(l3["carry"], 1)
                    dve.wait_ge(l3["carry"], l3.at("carry", n))
                    V.tensor_tensor(f(w["xhs"][:])[:, 1:G], f(w["hraw"][:])[:, 1:G], f(M[:])[:, 0:G - 1], ALU.add)
                    V.tensor_tensor(f(w["xhs"][:])[:, 0:1], f(w["hraw"][:])[:, 0:1], f(w["xh2"][:])[:, 0:1], ALU.add).then_inc(l3["e1"], 1)
                    dve.wait_ge(l3["e1"], l3.at("e1", n))
                    V.tensor_tensor(f(w["x1"][:]), f(w["xhs"][:]), f(M[:]), ALU.subtract).then_inc(l3["e2"], 1)
                    V.tensor_tensor(f(w["xh2"][:]), f(w["ms"][:]), f(M[:]), ALU.subtract).then_inc(l3["lm"], 1)
                if q is not None:
                    dve.wait_ge(l3["mk"], l3.at("mk", q.n))
                    dve.wait_ge(l3["q"], l3.at("q", q.n))
                    ge(dve, l3["ml"], l3.at("ml", q.n - 1))
                    V.scalar_tensor_tensor(out=f(w["msg"][:]), in0=pm2[:], scalar=col["bk"], in1=f(w["r"][:]),
                                           op0=ALU.add, op1=ALU.mult).then_inc(l3["qk"], 1)
                if mi is not None:
                    dve.wait_ge(l3["p"], l3.at("p", n))
                    dve.wait_ge(l3["mv"], l3.at("mv", n))
                    V.scalar_tensor_tensor(out=f(s2b[:, 0]), in0=pm3[0][:], scalar=col["bv"], in1=f(w["xc"][:]),
                                           op0=ALU.add, op1=ALU.mult).then_inc(l3["num"], 1)
                    num, numb = nums[mi.b], nums[1 - mi.b]
                    den, denb = dens[mi.b], dens[1 - mi.b]
                    dve.wait_ge(l3["num"], l3.at("num", n))
                    ge(dve, l3["tn"], l3.at("tn", n - 2))
                    V.tensor_tensor_scan(f(num), f(w["xb"][:]), f(s2b[:, 0]), 0.0 if first else numb[:, R - 1, D - 1:D],
                                         ALU.mult, ALU.add).then_inc(l3["nsc"], 1)
                    V.tensor_tensor_scan(f(den), f(w["xb"][:]), f(w["xc"][:]), 0.0 if first else denb[:, R - 1, D - 1:D],
                                         ALU.mult, ALU.add).then_inc(l3["den"], 1)
                if ba is not None:
                    dve.wait_ge(l3["tn"], l3.at("tn", ba.n))
                    V.reciprocal(sm[:, 5, :], pT2[:, 0:R]).then_inc(l3["rc"], 1)
                    dve.wait_ge(l3["rc"], l3.at("rc", ba.n))
                    for r in range(R):
                        last = V.scalar_tensor_tensor(out=ub[:, ba.b, r, :], in0=pG[:, r * D:(r + 1) * D], scalar=sm[:, 5, r:r + 1],
                                                      in1=bases[ba.b][:, r, :], op0=ALU.mult, op1=ALU.add)
                    last.then_inc(l3["z"], 1)
                    dve.wait_ge(l3["z"], l3.at("z", ba.n))
                    ge(dve, l3["out"], l3.at("out", ba.n - 1))
                    stats(lambda r: ub[:, ba.b, r, :], 1, l3["var"], ba.n)
                    variance(vin2[:], 1).then_inc(l3["var"], 1)
                if q is not None:
                    dve.wait_ge(l3["mm"], l3.at("mm", q.n))
                    V.tensor_tensor(bases[q.b], pm4[:].rearrange("p (r d) -> p r d", r=R),
                                    X[:, span(q.g * R, R), :], ALU.add).then_inc(l3["base"], 1)
            passes(V.Fori, "E", 3, l3_step)


_INS = ["x", "src", "dst", "edge_attr_128", "L0_gnn_g1", "L0_gnn_b1", "L0_gnn_g2", "L0_gnn_b2", "L0_gnn_eps_gin",
        "L0_gnn_Wg1", "L0_gnn_bg1", "L0_gnn_Wg2", "L0_gnn_bg2", "L0_gnn_Wf1", "L0_gnn_bf1", "L0_gnn_Wf2",
        "L0_gnn_bf2", "L1_gnn_eps", "L2_gnn_eps", "L2_gnn_W1", "L2_gnn_b1", "L2_gnn_gamma", "L2_gnn_beta",
        "L2_gnn_W2", "L2_gnn_b2", "L3_gnn_Wq", "L3_gnn_bq", "L3_gnn_Wk", "L3_gnn_bk", "L3_gnn_Wv", "L3_gnn_bv",
        "L3_gnn_Wskip", "L3_gnn_bskip"]


def kernel(**inputs):
    import numpy as _np
    import concourse.bacc as _bacc
    from concourse import mybir as _mybir
    from concourse.bass_utils import run_bass_kernel_spmd as _run

    nc = _bacc.Bacc("TRN2", target_bir_lowering=False, num_devices=1)
    arrays, args = {}, {}
    for name in _INS:
        v = _np.ascontiguousarray(inputs[name])
        v = v.reshape(v.shape or (1,))
        arrays[f"in_{name}_dram"] = v
        args[name] = nc.dram_tensor(f"in_{name}_dram", v.shape, _mybir.dt.from_np(v.dtype), kind="ExternalInput").ap()
    args["out"] = nc.dram_tensor("out_dram", (N, D), F32, kind="ExternalOutput").ap()
    build(nc, args)
    r = _run(nc, [arrays], core_ids=[0])
    return r.results[0]["out_dram"]
```
